# Optimizing a Trainium2 kernel written in Bass

```python
import numpy as np
import jax
import jax.numpy as jnp

def _softmax(x, axis=-1):
    return jax.nn.softmax(x, axis=axis)

def _gelu(x):
    return jax.nn.gelu(x, approximate=True)

def _silu(x):
    return jax.nn.silu(x)

def _sigmoid(x):
    return jax.nn.sigmoid(x)

def _layernorm(x, axis=-1, eps=1e-05):
    m = jnp.mean(x, axis=axis, keepdims=True)
    v = jnp.var(x, axis=axis, keepdims=True)
    return (x - m) / jnp.sqrt(v + eps)

def _scatter_add(tgt, idx, src, axis=0):
    return tgt.at[idx].add(src)

def _segment_sum(src, seg, n):
    return jax.ops.segment_sum(src, seg, n)
kernel_name = 'mk_decoder_postln_d1_seqx_r8_f72ed7'

def setup_inputs(seed: int=0):
    np.random.seed(seed)
    _w = jnp.asarray

    def _rec_inputs():
        import jax
        import jax.numpy as jnp
        _rk = jax.random.key(seed)
        x = 7.22e-05 + 1 * jax.random.normal(jax.random.fold_in(_rk, 1), (16, 64, 128), jnp.float32)
        _lenS = 64 - jax.random.randint(jax.random.fold_in(_rk, 7), (16,), 0, max(1, 64 // 4) + 1, jnp.int32)
        _lenS2 = 64 - jax.random.randint(jax.random.fold_in(_rk, 8), (16,), 0, max(1, 64 // 4) + 1, jnp.int32)
        _ctx_1024P = jax.random.normal(jax.random.fold_in(_rk, 11), (16, 16, 128), jnp.float32)
        _ctx_1024c = jax.random.dirichlet(jax.random.fold_in(_rk, 511), 0.3 * jnp.ones((16,), jnp.float32), (16, 64))
        _ctx_1024t = jnp.einsum('bsk,bkd->bsd', _ctx_1024c, _ctx_1024P)
        _ctx_1024t = _ctx_1024t * jax.lax.rsqrt(jnp.mean(jnp.square(_ctx_1024t)) + 1e-12) * 0.953939
        ctx_1024 = 4.13588e-05 + 0.999923 * (_ctx_1024t + 0.3 * jax.random.normal(jax.random.fold_in(_rk, 611), (16, 64, 128), jnp.float32))
        return (x, ctx_1024)
    x, ctx_1024 = _rec_inputs()

    def _L0_attn_setup():
        import jax, jax.numpy as jnp
        import numpy as np
        EMBED_DIM = 128
        NUM_HEAD = 16
        NEG_BIG = 10000000000.0
        key = jax.random.key(seed)
        k_x, k_w1, k_b1, k_w2, k_b2 = jax.random.split(key, 5)
        B, S, E = (4, 256, EMBED_DIM)
        std = 1.0 / np.sqrt(E)
        return {'x': jax.random.normal(k_x, (B, S, E), dtype=jnp.float32), 'W1': jax.random.uniform(k_w1, (E, 3 * E), dtype=jnp.float32, minval=-std, maxval=std), 'b1': jax.random.uniform(k_b1, (3 * E,), dtype=jnp.float32, minval=-std, maxval=std), 'W2': jax.random.uniform(k_w2, (E, E), dtype=jnp.float32, minval=-std, maxval=std), 'b2': jax.random.uniform(k_b2, (E,), dtype=jnp.float32, minval=-std, maxval=std)}
    _L0_attn_all = _L0_attn_setup()
    _L0_attn_in = {k: v for k, v in _L0_attn_all.items() if k in ('W1', 'b1', 'W2', 'b2')}
    del _L0_attn_all

    def _L0_xattn_setup():
        import jax, jax.numpy as jnp
        import numpy as np
        EMBED = 128
        HEADS = 16
        HEAD_DIM = EMBED // HEADS
        WINDOW = 128
        HALF = WINDOW // 2
        SCALE = HEAD_DIM ** (-0.5)
        B, T = (2, 512)

        def _sliding_window_attn(q, k, v):
            Bq, H, Tq, D = q.shape
            Bk = HALF
            nb = Tq // Bk
            qb = q.reshape(Bq, H, nb, Bk, D)

            def ctx(x):
                xb = x.reshape(Bq, H, nb, Bk, D)
                prev = jnp.concatenate([jnp.zeros_like(xb[:, :, :1]), xb[:, :, :-1]], axis=2)
                return jnp.concatenate([prev, xb], axis=3)
            kc, vc = (ctx(k), ctx(v))
            scores = jnp.einsum('bhnrd,bhncd->bhnrc', qb, kc)
            r = jnp.arange(Bk)[:, None]
            c = jnp.arange(2 * Bk)[None, :]
            band = (c >= r) & (c <= r + Bk)
            b_idx = jnp.arange(nb)[:, None, None]
            valid = band[None] & ((b_idx > 0) | (c[None] >= Bk))
            neg_inf = jnp.finfo(jnp.float32).min
            scores = jnp.where(valid[None, None], scores.astype(jnp.float32), neg_inf)
            attn = jax.nn.softmax(scores, axis=-1).astype(q.dtype)
            out = jnp.einsum('bhnrc,bhncd->bhnrd', attn, vc)
            return out.reshape(Bq, H, Tq, D)
        key = jax.random.key(seed)
        ks = jax.random.split(key, 11)
        f = jnp.float32
        return {'query': jax.random.normal(ks[0], (B, T, EMBED), f), 'key': jax.random.normal(ks[1], (B, T, EMBED), f), 'value': jax.random.normal(ks[2], (B, T, EMBED), f), 'wq': jax.random.normal(ks[3], (EMBED, EMBED), f) * 0.02, 'bq': jax.random.normal(ks[4], (EMBED,), f) * 0.02, 'wk': jax.random.normal(ks[5], (EMBED, EMBED), f) * 0.02, 'bk': jax.random.normal(ks[6], (EMBED,), f) * 0.02, 'wv': jax.random.normal(ks[7], (EMBED, EMBED), f) * 0.02, 'bv': jax.random.normal(ks[8], (EMBED,), f) * 0.02, 'wo': jax.random.normal(ks[9], (EMBED, EMBED), f) * 0.02, 'bo': jax.random.normal(ks[10], (EMBED,), f) * 0.02}
    _L0_xattn_all = _L0_xattn_setup()
    _L0_xattn_in = {k: v for k, v in _L0_xattn_all.items() if k in ('wq', 'bq', 'wk', 'bk', 'wv', 'bv', 'wo', 'bo')}
    del _L0_xattn_all

    def _L0_ffn_setup():
        import jax, jax.numpy as jnp
        import numpy as np
        D_MODEL = 128
        N_HEADS = 16
        N_GROUPS = 4
        D_FF = 512
        N_EXPERTS = 8
        TOP_K = 2
        BATCH = 2
        SEQ = 128
        D_K = D_MODEL // N_HEADS
        HPG = N_HEADS // N_GROUPS
        EPS = 1e-06

        def rms_norm(x, w):
            rms = jnp.sqrt(jnp.mean(x * x, axis=-1, keepdims=True) + EPS)
            return x / rms * w

        def rope(x):
            d = x.shape[-1]
            half = d // 2
            theta = 1.0 / 10000.0 ** (jnp.arange(half, dtype=jnp.float32) / half)
            pos = jnp.arange(x.shape[1], dtype=jnp.float32)[:, None]
            ang = pos * theta[None, :]
            cos, sin = (jnp.cos(ang), jnp.sin(ang))
            xe, xo = (x[..., 0::2], x[..., 1::2])
            return jnp.concatenate([xe * cos - xo * sin, xe * sin + xo * cos], axis=-1)

        def attention(x, Wq, Wk, Wv, Wo):
            B, S, _ = x.shape
            xr = rope(x)
            Q = (xr @ Wq).reshape(B, S, N_HEADS, D_K).transpose(0, 2, 1, 3)
            Q = Q.reshape(B, N_GROUPS, HPG, S, D_K)
            K = (xr @ Wk).reshape(B, S, N_GROUPS, D_K).transpose(0, 2, 1, 3)
            V = (xr @ Wv).reshape(B, S, N_GROUPS, D_K).transpose(0, 2, 1, 3)
            scores = jnp.einsum('bghsd,bgtd->bghst', Q, K) / jnp.sqrt(jnp.float32(D_K))
            mask = jnp.triu(jnp.full((S, S), -1000000000.0, dtype=scores.dtype), k=1)
            attn = jax.nn.softmax(scores + mask, axis=-1)
            out = jnp.einsum('bghst,bgtd->bghsd', attn, V)
            out = out.reshape(B, N_HEADS, S, D_K).transpose(0, 2, 1, 3).reshape(B, S, D_MODEL)
            return out @ Wo

        def moe(x, router_w, router_b, W1, b1, W2, b2, W3, b3):
            B, S, _ = x.shape
            logits = x @ router_w + router_b
            topv, topi = jax.lax.top_k(logits, TOP_K)
            topw = jax.nn.softmax(topv, axis=-1)
            onehot = jax.nn.one_hot(topi, N_EXPERTS, dtype=x.dtype)
            comb = jnp.einsum('bsk,bske->bse', topw, onehot)
            h1 = jnp.einsum('bsd,edf->ebsf', x, W1) + b1[:, None, None, :]
            h2 = jnp.einsum('bsd,edf->ebsf', x, W2) + b2[:, None, None, :]
            h = h2 * jax.nn.silu(h1)
            eo = jnp.einsum('ebsf,efd->ebsd', h, W3) + b3[:, None, None, :]
            return jnp.einsum('bse,ebsd->bsd', comb, eo)
        key = jax.random.key(seed)
        ks = jax.random.split(key, 16)
        s = 0.02
        return {'x': jax.random.normal(ks[0], (BATCH, SEQ, D_MODEL), dtype=jnp.float32), 'norm1_w': jnp.ones((D_MODEL,), jnp.float32), 'Wq': jax.random.normal(ks[1], (D_MODEL, D_MODEL), jnp.float32) * s, 'Wk': jax.random.normal(ks[2], (D_MODEL, N_GROUPS * D_K), jnp.float32) * s, 'Wv': jax.random.normal(ks[3], (D_MODEL, N_GROUPS * D_K), jnp.float32) * s, 'Wo': jax.random.normal(ks[4], (D_MODEL, D_MODEL), jnp.float32) * s, 'norm2_w': jnp.ones((D_MODEL,), jnp.float32), 'router_w': jax.random.normal(ks[5], (D_MODEL, N_EXPERTS), jnp.float32) * s, 'router_b': jnp.zeros((N_EXPERTS,), jnp.float32), 'W1': jax.random.normal(ks[6], (N_EXPERTS, D_MODEL, D_FF), jnp.float32) * s, 'b1': jnp.zeros((N_EXPERTS, D_FF), jnp.float32), 'W2': jax.random.normal(ks[7], (N_EXPERTS, D_MODEL, D_FF), jnp.float32) * s, 'b2': jnp.zeros((N_EXPERTS, D_FF), jnp.float32), 'W3': jax.random.normal(ks[8], (N_EXPERTS, D_FF, D_MODEL), jnp.float32) * s, 'b3': jnp.zeros((N_EXPERTS, D_MODEL), jnp.float32)}
    _L0_ffn_all = _L0_ffn_setup()
    _L0_ffn_in = {k: v for k, v in _L0_ffn_all.items() if k in ('norm1_w', 'Wq', 'Wk', 'Wv', 'Wo', 'norm2_w', 'router_w', 'router_b', 'W1', 'b1', 'W2', 'b2', 'W3', 'b3')}
    del _L0_ffn_all
    return {'x': x, 'ctx_1024': ctx_1024, 'L0_attn_W1': _L0_attn_in['W1'], 'L0_attn_b1': _L0_attn_in['b1'], 'L0_attn_W2': _L0_attn_in['W2'], 'L0_attn_b2': _L0_attn_in['b2'], 'L0_xattn_wq': _L0_xattn_in['wq'], 'L0_xattn_bq': _L0_xattn_in['bq'], 'L0_xattn_wk': _L0_xattn_in['wk'], 'L0_xattn_bk': _L0_xattn_in['bk'], 'L0_xattn_wv': _L0_xattn_in['wv'], 'L0_xattn_bv': _L0_xattn_in['bv'], 'L0_xattn_wo': _L0_xattn_in['wo'], 'L0_xattn_bo': _L0_xattn_in['bo'], 'L0_ffn_norm1_w': _L0_ffn_in['norm1_w'], 'L0_ffn_Wq': _L0_ffn_in['Wq'], 'L0_ffn_Wk': _L0_ffn_in['Wk'], 'L0_ffn_Wv': _L0_ffn_in['Wv'], 'L0_ffn_Wo': _L0_ffn_in['Wo'], 'L0_ffn_norm2_w': _L0_ffn_in['norm2_w'], 'L0_ffn_router_w': _L0_ffn_in['router_w'], 'L0_ffn_router_b': _L0_ffn_in['router_b'], 'L0_ffn_W1': _L0_ffn_in['W1'], 'L0_ffn_b1': _L0_ffn_in['b1'], 'L0_ffn_W2': _L0_ffn_in['W2'], 'L0_ffn_b2': _L0_ffn_in['b2'], 'L0_ffn_W3': _L0_ffn_in['W3'], 'L0_ffn_b3': _L0_ffn_in['b3']}

def reference(x, ctx_1024, L0_attn_W1, L0_attn_b1, L0_attn_W2, L0_attn_b2, L0_xattn_wq, L0_xattn_bq, L0_xattn_wk, L0_xattn_bk, L0_xattn_wv, L0_xattn_bv, L0_xattn_wo, L0_xattn_bo, L0_ffn_norm1_w, L0_ffn_Wq, L0_ffn_Wk, L0_ffn_Wv, L0_ffn_Wo, L0_ffn_norm2_w, L0_ffn_router_w, L0_ffn_router_b, L0_ffn_W1, L0_ffn_b1, L0_ffn_W2, L0_ffn_b2, L0_ffn_W3, L0_ffn_b3):
    import jax
    import jax.numpy as jnp

    def _L0_attn_ref(x, W1, b1, W2, b2):
        import jax, jax.numpy as jnp
        import numpy as np
        EMBED_DIM = 128
        NUM_HEAD = 16
        NEG_BIG = 10000000000.0
        B, S, E = x.shape
        H = NUM_HEAD
        y = jnp.einsum('bse,ef->bsf', x, W1) + b1
        y = y.reshape(B, S, H, -1).transpose(0, 2, 1, 3)
        q, k, v = jnp.split(y, 3, axis=-1)
        dk = jnp.asarray(v.shape[-1], x.dtype) ** 0.5
        w = jnp.einsum('bhqd,bhkd->bhqk', q, k) / dk
        mask = jnp.tril(jnp.ones((S, S), dtype=x.dtype))
        w = w * mask - NEG_BIG * (1.0 - mask)
        w = jax.nn.softmax(w, axis=-1)
        attn = jnp.einsum('bhqk,bhkd->bhqd', w, v)
        attn = attn.transpose(0, 2, 1, 3).reshape(B, S, E)
        return jnp.einsum('bse,ef->bsf', attn, W2) + b2

    def _L0_xattn_ref(query, key, value, wq, bq, wk, bk, wv, bv, wo, bo):
        import jax, jax.numpy as jnp
        import numpy as np
        EMBED = 128
        HEADS = 16
        HEAD_DIM = EMBED // HEADS
        WINDOW = 128
        HALF = WINDOW // 2
        SCALE = HEAD_DIM ** (-0.5)
        B, T = (2, 512)

        def _sliding_window_attn(q, k, v):
            Bq, H, Tq, D = q.shape
            Bk = HALF
            nb = Tq // Bk
            qb = q.reshape(Bq, H, nb, Bk, D)

            def ctx(x):
                xb = x.reshape(Bq, H, nb, Bk, D)
                prev = jnp.concatenate([jnp.zeros_like(xb[:, :, :1]), xb[:, :, :-1]], axis=2)
                return jnp.concatenate([prev, xb], axis=3)
            kc, vc = (ctx(k), ctx(v))
            scores = jnp.einsum('bhnrd,bhncd->bhnrc', qb, kc)
            r = jnp.arange(Bk)[:, None]
            c = jnp.arange(2 * Bk)[None, :]
            band = (c >= r) & (c <= r + Bk)
            b_idx = jnp.arange(nb)[:, None, None]
            valid = band[None] & ((b_idx > 0) | (c[None] >= Bk))
            neg_inf = jnp.finfo(jnp.float32).min
            scores = jnp.where(valid[None, None], scores.astype(jnp.float32), neg_inf)
            attn = jax.nn.softmax(scores, axis=-1).astype(q.dtype)
            out = jnp.einsum('bhnrc,bhncd->bhnrd', attn, vc)
            return out.reshape(Bq, H, Tq, D)
        Bq, Tq, C = query.shape
        split = lambda x: x.reshape(Bq, Tq, HEADS, HEAD_DIM).transpose(0, 2, 1, 3)
        q = split(jnp.einsum('btc,oc->bto', query, wq) + bq) * SCALE
        k = split(jnp.einsum('btc,oc->bto', key, wk) + bk)
        v = split(jnp.einsum('btc,oc->bto', value, wv) + bv)
        o = _sliding_window_attn(q, k, v)
        o = o.transpose(0, 2, 1, 3).reshape(Bq, Tq, C)
        return jnp.einsum('btc,oc->bto', o, wo) + bo

    def _L0_ffn_ref(x, norm1_w, Wq, Wk, Wv, Wo, norm2_w, router_w, router_b, W1, b1, W2, b2, W3, b3):
        import jax, jax.numpy as jnp
        import numpy as np
        D_MODEL = 128
        N_HEADS = 16
        N_GROUPS = 4
        D_FF = 512
        N_EXPERTS = 8
        TOP_K = 2
        BATCH = 2
        SEQ = 128
        D_K = D_MODEL // N_HEADS
        HPG = N_HEADS // N_GROUPS
        EPS = 1e-06

        def rms_norm(x, w):
            rms = jnp.sqrt(jnp.mean(x * x, axis=-1, keepdims=True) + EPS)
            return x / rms * w

        def rope(x):
            d = x.shape[-1]
            half = d // 2
            theta = 1.0 / 10000.0 ** (jnp.arange(half, dtype=jnp.float32) / half)
            pos = jnp.arange(x.shape[1], dtype=jnp.float32)[:, None]
            ang = pos * theta[None, :]
            cos, sin = (jnp.cos(ang), jnp.sin(ang))
            xe, xo = (x[..., 0::2], x[..., 1::2])
            return jnp.concatenate([xe * cos - xo * sin, xe * sin + xo * cos], axis=-1)

        def attention(x, Wq, Wk, Wv, Wo):
            B, S, _ = x.shape
            xr = rope(x)
            Q = (xr @ Wq).reshape(B, S, N_HEADS, D_K).transpose(0, 2, 1, 3)
            Q = Q.reshape(B, N_GROUPS, HPG, S, D_K)
            K = (xr @ Wk).reshape(B, S, N_GROUPS, D_K).transpose(0, 2, 1, 3)
            V = (xr @ Wv).reshape(B, S, N_GROUPS, D_K).transpose(0, 2, 1, 3)
            scores = jnp.einsum('bghsd,bgtd->bghst', Q, K) / jnp.sqrt(jnp.float32(D_K))
            mask = jnp.triu(jnp.full((S, S), -1000000000.0, dtype=scores.dtype), k=1)
            attn = jax.nn.softmax(scores + mask, axis=-1)
            out = jnp.einsum('bghst,bgtd->bghsd', attn, V)
            out = out.reshape(B, N_HEADS, S, D_K).transpose(0, 2, 1, 3).reshape(B, S, D_MODEL)
            return out @ Wo

        def moe(x, router_w, router_b, W1, b1, W2, b2, W3, b3):
            B, S, _ = x.shape
            logits = x @ router_w + router_b
            topv, topi = jax.lax.top_k(logits, TOP_K)
            topw = jax.nn.softmax(topv, axis=-1)
            onehot = jax.nn.one_hot(topi, N_EXPERTS, dtype=x.dtype)
            comb = jnp.einsum('bsk,bske->bse', topw, onehot)
            h1 = jnp.einsum('bsd,edf->ebsf', x, W1) + b1[:, None, None, :]
            h2 = jnp.einsum('bsd,edf->ebsf', x, W2) + b2[:, None, None, :]
            h = h2 * jax.nn.silu(h1)
            eo = jnp.einsum('ebsf,efd->ebsd', h, W3) + b3[:, None, None, :]
            return jnp.einsum('bse,ebsd->bsd', comb, eo)
        h = x + attention(rms_norm(x, norm1_w), Wq, Wk, Wv, Wo)
        h = h + moe(rms_norm(h, norm2_w), router_w, router_b, W1, b1, W2, b2, W3, b3)
        return h
    x = _layernorm(x + _L0_attn_ref(x, L0_attn_W1, L0_attn_b1, L0_attn_W2, L0_attn_b2), axis=-1)
    x = _layernorm(x + _L0_xattn_ref(x, ctx_1024, ctx_1024, L0_xattn_wq, L0_xattn_bq, L0_xattn_wk, L0_xattn_bk, L0_xattn_wv, L0_xattn_bv, L0_xattn_wo, L0_xattn_bo), axis=-1)
    x = _layernorm(x + _L0_ffn_ref(x, L0_ffn_norm1_w, L0_ffn_Wq, L0_ffn_Wk, L0_ffn_Wv, L0_ffn_Wo, L0_ffn_norm2_w, L0_ffn_router_w, L0_ffn_router_b, L0_ffn_W1, L0_ffn_b1, L0_ffn_W2, L0_ffn_b2, L0_ffn_W3, L0_ffn_b3), axis=-1)
    return x

_drawn_inputs = setup_inputs


def setup_inputs(seed=0):
    import zlib

    import numpy as np

    out = dict(_drawn_inputs(seed))
    spreads = {'L0_ffn_norm1_w': (1.0, 0.6),
     'L0_ffn_norm2_w': (1.0, 0.6),
     'L0_ffn_router_b': (0.0, 0.442),
     'L0_ffn_b1': (0.0, 0.8),
     'L0_ffn_b2': (0.0, 0.8),
     'L0_ffn_b3': (0.0, 0.8)}
    factors = {'L0_xattn_wq': 8.0,
     'L0_xattn_bq': 8.0,
     'L0_xattn_wk': 8.0,
     'L0_xattn_bk': 64.0,
     'L0_xattn_bv': 8.0,
     'L0_ffn_Wq': 8.0,
     'L0_ffn_Wk': 8.0,
     'L0_ffn_Wv': 6.865,
     'L0_ffn_Wo': 6.655,
     'L0_ffn_W1': 8.0,
     'L0_ffn_W2': 8.0,
     'L0_ffn_W3': 8.0}
    for name, (base, spread) in spreads.items():
        noise = np.random.default_rng([zlib.crc32(name.encode()), seed]).standard_normal(out[name].shape)
        drawn = base * np.exp(spread * noise) if base else spread * noise
        out[name] = jnp.asarray(drawn.astype(out[name].dtype))
    for name, factor in factors.items():
        out[name] = (out[name] * factor).astype(out[name].dtype)
    return out
```

```python
from contextlib import ExitStack

import numpy as np

import concourse.bass as bass
from concourse import mybir

F32 = mybir.dt.float32
BF16 = mybir.dt.bfloat16
ALU = mybir.AluOpType
ACT = mybir.ActivationFunctionType
AX = mybir.AxisListType

P = 128
D = 128
S = 64
B = 16
NT = B * S // P
HD = 8
NP = 8
FF = 512
NE = 8
SCALE = float(HD) ** -0.5
STAGES = 3
STEPS = STAGES * NT
RT_EXP = 13
LN_EPS = 1e-5
RMS_EPS = 1e-6
C_ID, C_I2, C_MASK, C_COS, C_SIN, C_MA, C_M8, C_END = 0, 128, 192, 704, 832, 960, 962, 970


def decoder_kernel(nc, t_in, consts, out):
    ctx = ExitStack()
    with ctx:
        def sb(name, shape, dt=F32):
            return ctx.enter_context(nc.sbuf_tensor(name, shape, dt))

        def sem(name):
            return ctx.enter_context(nc.semaphore(name))

        bank = [ctx.enter_context(nc.psum_tensor(f"bank{i}", [P, 512], F32)) for i in range(8)]
        ps_score = [bank[0], bank[1]]
        ps_pt = [bank[2], bank[3]]
        ps_xt, ps_qkv, ps_o, ps_y = bank[4], bank[5], bank[6], bank[7]
        ps_v = ps_xt[:, 2 * P:3 * P]

        cst = sb("cst", [P, C_END])
        ident = cst[:, C_ID:C_ID + P]
        fold2 = cst[:, C_I2:C_I2 + S]
        mask_a = cst[:, C_MA:C_MA + 2]
        mask_p = cst[:, C_M8:C_M8 + NP]
        ident_bf = sb("ident_bf", [P, P], BF16)
        mask_bf = sb("mask_bf", [P, 512], BF16)
        ones_bf = sb("ones_bf", [3, P], BF16)
        x_tok = sb("x_tok", [P, NT, D])
        c_tok = sb("c_tok", [P, NT, D])
        x1 = sb("x1", [P, NT, D])
        x2 = sb("x2", [P, NT, D])
        xr = sb("xr", [P, NT, D])
        h3 = sb("h3", [P, NT, D])
        res_b = sb("res_b", [P, 2, NT, D])
        w_raw = sb("w_raw", [P, 3 * D])
        wx_raw = sb("wx_raw", [P, 4, D])
        wkv_raw = sb("wkv_raw", [P, 2, 32])
        w_q = sb("w_q", [P, 3, D])
        w_k = sb("w_k", [P, 3, D])
        w_v = sb("w_v", [P, 3, D])
        w_o = sb("w_o", [P, 3, D])
        bias_col = sb("bias_col", [P, 3, 3])
        bias_qa = sb("bias_qa", [P, 3, 2])
        bias_row = sb("bias_row", [P, 2, D])
        w_norm = sb("w_norm", [P, 2, D])
        rope_c = sb("rope_c", [P, D])
        rope_s = sb("rope_s", [P, D])
        xt = sb("xt", [P, 2, 2, P])
        q2 = sb("q2", [P, 2, 2, 2, S])
        kt = sb("kt", [P, 2, P])
        k2 = sb("k2", [P, 2, 2, NP, S])
        vbd = sb("vbd", [P, 2, 2, 4, 2, 17])
        s_sb = sb("s_sb", [P, 2, 512])
        p_sb = sb("p_sb", [P, 2, 512])
        pt_sb = sb("pt_sb", [P, 2, 512])
        smax = sb("smax", [P, 2, NP])
        rsum = sb("rsum", [P, 2, 2 * NP])
        o_sb = sb("o_sb", [P, 2, 2, NP, 2, HD])
        ot_sb = sb("ot_sb", [P, 2, P])
        res = sb("res", [P, 2, D])
        stats = sb("stats", [P, 2, 6])
        mv = sb("mv", [P, 2, 2])
        rstd = sb("rstd", [P, 2, 4])
        half_neg = sb("half_neg", [P, 1])
        rope_a = sb("rope_a", [P, D])
        rope_b = sb("rope_b", [P, D])
        sq = sb("sq", [P, D])
        w1 = sb("w1", [P, NE, FF])
        w2 = sb("w2", [P, NE, FF])
        w3 = sb("w3", [P, NE, 4, D])
        rw = sb("rw", [P, NE])
        rb = sb("rb", [P, NE])
        b_raw = sb("b_raw", [NE, 2 * FF + D])
        b_hi = sb("b_hi", [NE, 2 * FF + D], BF16)
        b_mid = sb("b_mid", [NE, 2 * FF + D], BF16)
        b_lo = sb("b_lo", [NE, 2 * FF + D], BF16)
        b_r1 = sb("b_r1", [NE, 2 * FF + D])
        b_r2 = sb("b_r2", [NE, 2 * FF + D])
        b_row = sb("b_row", [3, NE, 2 * FF + D], BF16)
        xm = sb("xm", [P, NT, D])
        xmt = sb("xmt", [P, NT, D])
        logit = sb("logit", [P, NT, NE])
        rt = sb("rt", [P, 8, NT, NE])
        rv = sb("rv", [P, 8, NT])
        comb = sb("comb", [P, NT, NE])
        silu = sb("silu", [P, 2, FF])
        hh = sb("hh", [P, 2, FF])
        ht = sb("ht", [P, 2, FF])
        acc = sb("acc", [P, NT, D])
        fstats = sb("fstats", [P, NT, 6])
        fmv = sb("fmv", [P, NT, 2])
        frstd = sb("frstd", [P, NT, 2])
        base = sb("base", [P, NT, D])
        y_out = sb("y_out", [P, NT, D])

        in_cst = sem("in_cst")
        in_x = sem("in_x")
        in_ctx = sem("in_ctx")
        in_w = sem("in_w")
        in_wx = sem("in_wx")
        in_b = sem("in_b")
        in_w3rd = sem("in_w3rd")
        in_moe = sem("in_moe")
        in_brow = sem("in_brow")
        out_done = sem("out_done")
        c_base = sem("c_base")
        c_bf = sem("c_bf")
        c_wq = sem("c_wq")
        c_wxt = sem("c_wxt")
        c_zero = sem("c_zero")
        c_bqa = sem("c_bqa")
        c_rope = sem("c_rope")
        c_resb = sem("c_resb")
        c_bparts = sem("c_bparts")
        c_half = sem("c_half")
        pe_wx = sem("pe_wx")
        pe_xt = sem("pe_xt")
        pe_qkv = sem("pe_qkv")
        pe_s = sem("pe_s")
        pe_pt = sem("pe_pt")
        pe_o = sem("pe_o")
        pe_ot = sem("pe_ot")
        pe_y = sem("pe_y")
        a_wx = sem("a_wx")
        a_xt = sem("a_xt")
        a_q = sem("a_q")
        a_k = sem("a_k")
        a_p = sem("a_p")
        a_pt = sem("a_pt")
        a_ot = sem("a_ot")
        a_sq = sem("a_sq")
        d_mx = sem("d_mx")
        d_s = sem("d_s")
        d_v = sem("d_v")
        d_rs = sem("d_rs")
        d_o = sem("d_o")
        d_res = sem("d_res")
        d_st = sem("d_st")
        d_mv = sem("d_mv")
        d_x = sem("d_x")
        d_ra = sem("d_ra")
        d_xr = sem("d_xr")
        d_xm = sem("d_xm")
        g_k2 = sem("g_k2")
        g_rs = sem("g_rs")
        g_rq = sem("g_rq")
        d_fmv = sem("d_fmv")
        g_frs = sem("g_frs")
        pe_xmt = sem("pe_xmt")
        a_xmt = sem("a_xmt")
        pe_lg = sem("pe_lg")
        d_lg = sem("d_lg")
        d_rt = sem("d_rt")
        a_rt = sem("a_rt")
        pe_h = sem("pe_h")
        a_silu = sem("a_silu")
        d_hh = sem("d_hh")
        pe_ht = sem("pe_ht")
        a_ht = sem("a_ht")
        pe_e = sem("pe_e")
        d_acc = sem("d_acc")
        d_fin = sem("d_fin")

        block = ctx.enter_context(nc.Block())

        def rstd_sum(n):
            return mv[:, n % 2, 0:1]

        def cnt_rs(n):
            return n + 1 if n < NT else (NT + 2 * (n - NT + 1) if n < 2 * NT else 3 * NT + (n - 2 * NT + 1))

        @block.sync
        def _(sp):
            tiles = "(t c) s e -> (c s) t e"
            sp.dma_start(x_tok[:, :, :], t_in["x"].rearrange(tiles, c=2)).then_inc(in_x, 16)
            sp.dma_start(w_raw[:, :], t_in["L0_attn_W1"]).then_inc(in_w, 16)
            sp.dma_start(w_o[:, 0, :], t_in["L0_attn_W2"]).then_inc(in_w, 16)
            b1 = t_in["L0_attn_b1"].rearrange("(h c d) -> c h d", c=3, d=HD)
            for c in range(3):
                sp.dma_start(bias_col[:, 0, c:c + 1], b1[c].rearrange("h (d u) -> h d u", u=1)).then_inc(in_b, 16)
            for c, n in enumerate(("bq", "bk", "bv")):
                sp.dma_start(bias_col[:, 1, c:c + 1],
                             t_in["L0_xattn_" + n].rearrange("(d u) -> d u", u=1)).then_inc(in_b, 16)
            sp.dma_start(c_tok[:, :, :], t_in["ctx_1024"].rearrange(tiles, c=2)).then_inc(in_ctx, 16)
            sp.dma_start(w1[:, :, :], t_in["L0_ffn_W1"].rearrange("e d f -> d e f")).then_inc(in_moe, 16)
            sp.dma_start(w2[:, :, :], t_in["L0_ffn_W2"].rearrange("e d f -> d e f")).then_inc(in_moe, 16)
            for e in range(NE):
                sp.dma_start(w3[:, e, :, :],
                             t_in["L0_ffn_W3"][e].rearrange("(c f) d -> f c d", f=P)).then_inc(in_moe, 16)
            sp.dma_start(rw[:, :], t_in["L0_ffn_router_w"]).then_inc(in_moe, 16)
            sp.dma_start(rb[:, :], t_in["L0_ffn_router_b"].rearrange("(a e) -> a e", a=1)
                         .to_broadcast([P, NE])).then_inc(in_moe, 16)
            sp.wait_ge(c_bparts, 5)
            for k, part in enumerate((b_hi, b_mid, b_lo)):
                sp.dma_start(b_row[k:k + 1, :, :], part[:, :]).then_inc(in_brow, 16)
            for t in range(NT):
                sp.wait_ge(d_fin, t + 1)
                sp.dma_start(out.rearrange(tiles, c=2)[:, t, :], y_out[:, t, :]).then_inc(out_done, 16)
            sp.wait_ge(out_done, 16 * NT)

        MOE_LOADS = 16 * (2 + NE + 2)

        @block.gpsimd
        def _(pool):
            g = nc.gpsimd
            g.memset(half_neg[:, :], -0.5).then_inc(c_half, 1)
            pool.wait_ge(in_cst, 16)
            g.tensor_copy(ident_bf[:, :], ident).then_inc(c_bf, 1)
            g.tensor_copy(mask_bf[:, :], cst[:, C_MASK:C_MASK + 512]).then_inc(c_bf, 1)
            pool.wait_ge(in_w, 32)
            wv = w_raw[:, :].rearrange("e (h c d) -> e c h d", c=3, d=HD)
            for c, w in enumerate((w_q, w_k, w_v)):
                g.tensor_copy(w[:, 0, :].rearrange("e (h d) -> e h d", d=HD), wv[:, c]).then_inc(c_wq, 1)
            pool.wait_ge(in_b, 96)
            pool.wait_ge(c_zero, 6)
            for s in range(3):
                for a in range(2):
                    g.tensor_tensor(bias_qa[:, s, a:a + 1], bias_col[:, s, 0:1], mask_a[:, a:a + 1],
                                    ALU.mult).then_inc(c_bqa, 1)
            pool.wait_ge(in_x, 16)
            pool.wait_ge(in_w3rd, 16 * 11)
            g.tensor_tensor(res_b[:, 0, :, :], x_tok[:, :, :],
                            bias_row[:, 0:1, :].to_broadcast([P, NT, D]), ALU.add).then_inc(c_resb, 1)
            g.tensor_tensor(rope_c[:, :], cst[:, C_COS:C_COS + D], w_norm[:, 0, :], ALU.mult).then_inc(c_rope, 1)
            g.tensor_tensor(rope_s[:, :], cst[:, C_SIN:C_SIN + D], w_norm[:, 0, :], ALU.mult).then_inc(c_rope, 1)
            for i, w in enumerate((w_k, w_v)):
                g.tensor_copy(w[:, 2, :].rearrange("e (g r d) -> e g r d", r=4, d=HD),
                              wkv_raw[:, i, :].rearrange("e (g u d) -> e g u d", u=1, d=HD)
                              .to_broadcast([P, 4, 4, HD])).then_inc(c_wq, 1)
            g.tensor_copy(b_hi[:, :], b_raw[:, :]).then_inc(c_bparts, 1)
            pool.wait_ge(c_bparts, 1)
            g.tensor_tensor(b_r1[:, :], b_raw[:, :], b_hi[:, :], ALU.subtract).then_inc(c_bparts, 1)
            pool.wait_ge(c_bparts, 2)
            g.tensor_copy(b_mid[:, :], b_r1[:, :]).then_inc(c_bparts, 1)
            pool.wait_ge(c_bparts, 3)
            g.tensor_tensor(b_r2[:, :], b_r1[:, :], b_mid[:, :], ALU.subtract).then_inc(c_bparts, 1)
            pool.wait_ge(c_bparts, 4)
            g.tensor_copy(b_lo[:, :], b_r2[:, :]).then_inc(c_bparts, 1)

            def expand_keys(n):
                pool.wait_ge(a_k, n + 1)
                if n >= 2:
                    pool.wait_ge(pe_s, 2 * (n - 1))
                i = n % 2
                g.tensor_tensor(
                    k2[:, i, :, :, :],
                    kt[:, i, :].rearrange("c (b u k) -> c b u k", b=2, u=1).to_broadcast([P, 2, NP, S]),
                    mask_p.rearrange("c (v p u) -> c v p u", v=1, u=1).to_broadcast([P, 2, NP, S]),
                    ALU.mult).then_inc(g_k2, 1)

            links = [0]

            def link():
                links[0] += 1
                pool.wait_ge(g_rq, links[0])

            def row_scale(n):
                s, i = n // NT, n % 2
                r = rstd[:, i, :]
                if s < 2:
                    pool.wait_ge(d_mv, n + 1)
                    if n >= 2:
                        pool.wait_ge(d_x, n - 1)
                        if n - 2 >= NT:
                            pool.wait_ge(d_ra, 2 * (n - 2 - NT + 1))
                    g.tensor_scalar(r[:, 0:1], mv[:, i, 1:2], LN_EPS, None, ALU.add).then_inc(g_rq, 1)
                    link()
                    g.tensor_tensor(r[:, 1:2], r[:, 0:1], half_neg[:, :], ALU.pow).then_inc(g_rs, 1)
                    if s == 1:
                        pool.wait_ge(g_rs, cnt_rs(n) - 1)
                        g.tensor_tensor(r[:, 2:3], r[:, 1:2], r[:, 1:2], ALU.mult).then_inc(g_rq, 1)
                        link()
                        g.tensor_tensor(r[:, 2:3], r[:, 2:3], mv[:, i, 1:2], ALU.mult).then_inc(g_rq, 1)
                        link()
                        g.tensor_scalar(r[:, 2:3], r[:, 2:3], RMS_EPS, None, ALU.add).then_inc(g_rq, 1)
                        link()
                        g.tensor_tensor(r[:, 3:4], r[:, 2:3], half_neg[:, :], ALU.pow).then_inc(g_rs, 1)
                else:
                    pool.wait_ge(a_sq, n - 2 * NT + 1)
                    pool.wait_ge(d_ra, 2 * NT)
                    if n - 2 >= 2 * NT:
                        pool.wait_ge(d_xm, n - 2 - 2 * NT + 1)
                    g.tensor_scalar(r[:, 0:1], rstd_sum(n), 1.0 / D, RMS_EPS, ALU.mult, ALU.add).then_inc(g_rq, 1)
                    link()
                    g.tensor_tensor(r[:, 1:2], r[:, 0:1], half_neg[:, :], ALU.pow).then_inc(g_rs, 1)

            def add_bias(n):
                if n < NT:
                    pool.wait_ge(d_x, n + 1)
                    g.tensor_tensor(res_b[:, 1, n, :], x1[:, n, :], bias_row[:, 1, :], ALU.add).then_inc(c_resb, 1)

            for it in range(STEPS + 3):
                if it < STEPS:
                    expand_keys(it)
                if 2 <= it < STEPS + 2:
                    row_scale(it - 2)
                if 3 <= it:
                    add_bias(it - 3)

            for t in range(NT):
                pool.wait_ge(d_res, 2 * NT + t + 1)
                g.tensor_tensor(base[:, t, :], h3[:, t, :], x2[:, t, :], ALU.add).then_inc(c_base, 1)
            for t in range(NT):
                pool.wait_ge(d_fmv, t + 1)
                g.tensor_scalar(frstd[:, t, 0:1], fmv[:, t, 1:2], LN_EPS, None, ALU.add).then_inc(g_frs, 1)
                pool.wait_ge(g_frs, 2 * t + 1)
                g.tensor_tensor(frstd[:, t, 1:2], frstd[:, t, 0:1], half_neg[:, :], ALU.pow).then_inc(g_frs, 1)

        @block.tensor
        def _(pe):
            mm = nc.tensor.matmul

            def turn(o, i, idn):
                return mm(o, i, idn, start=True, stop=True, is_transpose=True)

            def turn_x(n):
                s, t = n // NT, n % NT
                if s == 0:
                    pe.wait_ge(in_x, 16)
                elif s == 1:
                    pe.wait_ge(d_x, t + 1)
                    pe.wait_ge(in_ctx, 16)
                else:
                    pe.wait_ge(d_xr, 2 * (t + 1))
                if n >= 1:
                    pe.wait_ge(a_xt, n)
                    pe.wait_ge(d_v, 4 * n)
                src = (x_tok, x1, xr)[s]
                m = turn(ps_xt[:, 0:P], src[:, t, :], ident)
                if s == 1:
                    m = turn(ps_xt[:, P:2 * P], c_tok[:, t, :], ident)
                m.then_inc(pe_xt, 1)

            def project(n):
                s, i = n // NT, n % 2
                pe.wait_ge(a_xt, n + 1)
                if n >= 1:
                    pe.wait_ge(a_q, 2 * n)
                    pe.wait_ge(a_k, n)
                    pe.wait_ge(d_v, 4 * n)
                if n == 0:
                    pe.wait_ge(c_wq, 3)
                if n == NT:
                    pe.wait_ge(a_wx, 1)
                if n == 2 * NT:
                    pe.wait_ge(c_wq, 5)
                kv = xt[:, i, 1 if s == 1 else 0, :]
                mm(ps_qkv[:, 0:P], w_q[:, s, :], xt[:, i, 0, :], start=True, stop=True)
                mm(ps_qkv[:, P:2 * P], w_k[:, s, :], kv, start=True, stop=True)
                mm(ps_v, kv, w_v[:, s, :], start=True, stop=True).then_inc(pe_qkv, 1)

            def scores(n, b):
                m, i = 2 * n + b, n % 2
                if b == 0:
                    pe.wait_ge(a_q, 2 * (n + 1))
                    pe.wait_ge(g_k2, n + 1)
                if m >= 2:
                    pe.wait_ge(d_s, m - 1)
                mm(ps_score[b][:, :], ident_bf[:, :], mask_bf[:, :], start=True, stop=False)
                mm(ps_score[b][:, :], q2[:, i, b, :, :].rearrange("c a q -> c (a q)"),
                   k2[:, i, b, :, :].rearrange("c p k -> c (p k)"), start=False, stop=True).then_inc(pe_s, 1)

            def turn_p(n, b):
                m = 2 * n + b
                pe.wait_ge(a_p, m + 1)
                if m >= 2:
                    pe.wait_ge(a_pt, m - 1)
                for j in range(4):
                    k = turn(ps_pt[b][:, j * P:(j + 1) * P], p_sb[:, b, j * P:(j + 1) * P], ident)
                k.then_inc(pe_pt, 1)

            def values(n, b):
                m, i = 2 * n + b, n % 2
                pe.wait_ge(a_pt, m + 1)
                if b == 0:
                    pe.wait_ge(d_v, 4 * (n + 1))
                    if n >= 1:
                        pe.wait_ge(d_o, 2 * n)
                for j in range(4):
                    c = b * 136 + j * 34
                    k = mm(ps_o[:, c:c + 34], pt_sb[:, b, j * P:(j + 1) * P],
                           vbd[:, i, b, j, :, :].rearrange("k p c -> k (p c)"), start=True, stop=True)
                k.then_inc(pe_o, 1)

            def turn_o(n):
                i = n % 2
                pe.wait_ge(d_o, 2 * (n + 1))
                if n >= 1:
                    pe.wait_ge(d_res, n)
                for b in range(2):
                    k = mm(ps_y[:, b * S:(b + 1) * S], o_sb[:, i, b, :, :, :].rearrange("q p a d -> q (p a d)"),
                           fold2, start=True, stop=True)
                k.then_inc(pe_ot, 1)

            def out_proj(n):
                s, i = n // NT, n % 2
                pe.wait_ge(a_ot, n + 1)
                mm(ps_y[:, P:2 * P], ot_sb[:, i, :], w_o[:, s, :], start=True, stop=True).then_inc(pe_y, 1)

            pe.wait_ge(in_cst, 16)
            turn_x(0)
            pe.wait_ge(c_bf, 2)
            project(0)
            pe.wait_ge(in_wx, 64)
            for c in range(4):
                k = turn(ps_pt[0][:, c * P:(c + 1) * P], wx_raw[:, c, :], ident)
            k.then_inc(pe_wx, 1)
            pe.wait_ge(a_wx, 1)
            for it in range(STEPS + 3):
                if it < STEPS:
                    scores(it, 0)
                    scores(it, 1)
                if it + 1 < STEPS:
                    turn_x(it + 1)
                if 1 <= it <= STEPS:
                    turn_p(it - 1, 0)
                    turn_p(it - 1, 1)
                if 2 <= it < STEPS + 2:
                    turn_o(it - 2)
                if it + 1 < STEPS:
                    project(it + 1)
                if 1 <= it <= STEPS:
                    values(it - 1, 0)
                    values(it - 1, 1)
                if 2 <= it < STEPS + 2:
                    out_proj(it - 2)

            for t in range(NT):
                pe.wait_ge(d_xm, t + 1)
                if t >= 1:
                    pe.wait_ge(a_xmt, t)
                turn(ps_xt[:, 0:P], xm[:, t, :], ident).then_inc(pe_xmt, 1)
                pe.wait_ge(a_xmt, t + 1)
                if t == 0:
                    pe.wait_ge(in_moe, MOE_LOADS)
                mm(ps_qkv[:, t * NE:(t + 1) * NE], xmt[:, t, :], rw[:, :], start=True, stop=True).then_inc(pe_lg, 1)

            ps_h1, ps_h2 = [bank[0], bank[2]], [bank[1], bank[3]]
            ps_ht, ps_e = bank[4], [bank[5], bank[6]]

            def up(i):
                t, e = i // NE, i % NE
                if i >= 2:
                    pe.wait_ge(d_hh, i - 1)
                for dst, w, c in ((ps_h1, w1, 0), (ps_h2, w2, FF)):
                    mm(dst[i % 2][:, :], ones_bf[:, :], b_row[:, e, c:c + FF], start=True, stop=False)
                    k = mm(dst[i % 2][:, :], xmt[:, t, :], w[:, e, :], start=False, stop=True)
                k.then_inc(pe_h, 1)

            def turn_h(i):
                pe.wait_ge(d_hh, i + 1)
                if i >= 1:
                    pe.wait_ge(a_ht, i)
                for c in range(4):
                    k = turn(ps_ht[:, c * P:(c + 1) * P], hh[:, i % 2, c * P:(c + 1) * P], ident)
                k.then_inc(pe_ht, 1)

            def down(i):
                e = i % NE
                pe.wait_ge(a_ht, i + 1)
                if i >= 2:
                    pe.wait_ge(d_acc, i - 1)
                dst = ps_e[i % 2][:, 0:D]
                mm(dst, ones_bf[:, :], b_row[:, e, 2 * FF:2 * FF + D], start=True, stop=False)
                for c in range(4):
                    k = mm(dst, ht[:, i % 2, c * P:(c + 1) * P], w3[:, e, c, :], start=False, stop=(c == 3))
                k.then_inc(pe_e, 1)

            pe.wait_ge(in_brow, 48)
            pe.wait_ge(d_lg, 1)
            N = NT * NE
            for i in range(N + 2):
                if i < N:
                    up(i)
                if 1 <= i <= N:
                    turn_h(i - 1)
                if i >= 2:
                    down(i - 2)

        @block.scalar
        def _(act):
            A = nc.scalar.activation
            act.dma_start(cst[:, :], consts).then_inc(in_cst, 16)
            for c, n in enumerate(("wq", "wk", "wv", "wo")):
                act.dma_start(wx_raw[:, c, :], t_in["L0_xattn_" + n]).then_inc(in_wx, 16)
            for r, n in ((bias_row[:, 0, :], "L0_attn_b2"), (bias_row[:, 1, :], "L0_xattn_bo"),
                         (w_norm[:, 0, :], "L0_ffn_norm1_w"), (w_norm[:, 1, :], "L0_ffn_norm2_w")):
                act.dma_start(r, t_in[n].rearrange("(a e) -> a e", a=1).to_broadcast([P, D])).then_inc(in_w3rd, 16)
            act.dma_start(w_q[:, 2, :], t_in["L0_ffn_Wq"]).then_inc(in_w3rd, 16)
            act.dma_start(w_o[:, 2, :], t_in["L0_ffn_Wo"]).then_inc(in_w3rd, 16)
            act.dma_start(wkv_raw[:, 0, :], t_in["L0_ffn_Wk"]).then_inc(in_w3rd, 16)
            act.dma_start(wkv_raw[:, 1, :], t_in["L0_ffn_Wv"]).then_inc(in_w3rd, 16)
            act.dma_start(b_raw[:, 0:FF], t_in["L0_ffn_b1"]).then_inc(in_w3rd, 16)
            act.dma_start(b_raw[:, FF:2 * FF], t_in["L0_ffn_b2"]).then_inc(in_w3rd, 16)
            act.dma_start(b_raw[:, 2 * FF:], t_in["L0_ffn_b3"]).then_inc(in_w3rd, 16)

            def copy_xt(n):
                act.wait_ge(pe_xt, n + 1)
                if n >= 2:
                    act.wait_ge(pe_qkv, n - 1)
                w = 2 if n // NT == 1 else 1
                A(xt[:, n % 2, 0:w, :].rearrange("c x t -> c (x t)"), ps_xt[:, 0:w * P], ACT.Copy).then_inc(a_xt, 1)

            def copy_qk(n):
                s, i = n // NT, n % 2
                act.wait_ge(pe_qkv, n + 1)
                if n == 0:
                    act.wait_ge(c_bqa, 6)
                if n >= 2:
                    act.wait_ge(pe_s, 2 * (n - 1))
                    act.wait_ge(g_k2, n - 1)
                A(kt[:, i, :], ps_qkv[:, P:2 * P], ACT.Identity, bias=bias_col[:, s, 1:2]).then_inc(a_k, 1)
                for a in range(2):
                    A(q2[:, i, :, a, :], ps_qkv[:, 0:P].rearrange("c (b q) -> c b q", b=2), ACT.Identity,
                      bias=bias_qa[:, s, a:a + 1], scale=mask_a[:, a:a + 1]).then_inc(a_q, 1)

            def exponent(n, b):
                m = 2 * n + b
                act.wait_ge(d_s, m + 1)
                if m >= 2:
                    act.wait_ge(pe_pt, m - 1)
                A(p_sb[:, b, :], s_sb[:, b, :], ACT.Exp, scale=SCALE).then_inc(a_p, 1)

            def copy_pt(n, b):
                m = 2 * n + b
                act.wait_ge(pe_pt, m + 1)
                if m >= 2:
                    act.wait_ge(pe_o, m - 1)
                A(pt_sb[:, b, :], ps_pt[b][:, :], ACT.Copy).then_inc(a_pt, 1)

            def copy_ot(n):
                s = n // NT
                act.wait_ge(pe_ot, n + 1)
                if n >= 2:
                    act.wait_ge(pe_y, n - 1)
                A(ot_sb[:, n % 2, :], ps_y[:, 0:P], ACT.Identity, bias=bias_col[:, s, 2:3]).then_inc(a_ot, 1)

            def square(n):
                t = n - 2 * NT
                act.wait_ge(d_res, n + 1)
                if t >= 1:
                    act.wait_ge(a_sq, t)
                if t >= 2:
                    act.wait_ge(g_rs, cnt_rs(n - 2))
                A(sq[:, :], h3[:, t, :], ACT.Square, accum_out=mv[:, n % 2, 0:1]).then_inc(a_sq, 1)

            copy_xt(0)
            act.wait_ge(in_cst, 16)
            copy_qk(0)
            act.wait_ge(pe_wx, 1)
            for c, w in enumerate((w_q, w_k, w_v, w_o)):
                k = A(w[:, 1, :], ps_pt[0][:, c * P:(c + 1) * P], ACT.Copy)
            k.then_inc(a_wx, 1)
            for it in range(STEPS + 3):
                if it - 3 >= 2 * NT:
                    square(it - 3)
                if it + 1 < STEPS:
                    copy_xt(it + 1)
                if 1 <= it <= STEPS:
                    copy_pt(it - 1, 0)
                    copy_pt(it - 1, 1)
                if 2 <= it < STEPS + 2:
                    copy_ot(it - 2)
                if it < STEPS:
                    exponent(it, 0)
                if it + 1 < STEPS:
                    copy_qk(it + 1)
                if it < STEPS:
                    exponent(it, 1)
            act.wait_ge(d_res, STEPS)
            for t in range(NT):
                act.wait_ge(pe_xmt, t + 1)
                A(xmt[:, t, :], ps_xt[:, 0:P], ACT.Copy).then_inc(a_xmt, 1)
            act.wait_ge(d_rt, RT_EXP)
            A(rv[:, 3, :], rv[:, 2, :], ACT.Exp).then_inc(a_rt, 1)
            N = NT * NE
            for i in range(N + 1):
                if i < N:
                    act.wait_ge(pe_h, i + 1)
                    if i >= 2:
                        act.wait_ge(d_hh, i - 1)
                    A(silu[:, i % 2, :], (bank[0], bank[2])[i % 2][:, :], ACT.Silu).then_inc(a_silu, 1)
                if i >= 1:
                    act.wait_ge(pe_ht, i)
                    if i >= 3:
                        act.wait_ge(pe_e, i - 2)
                    A(ht[:, (i - 1) % 2, :], bank[4][:, :], ACT.Copy).then_inc(a_ht, 1)

        @block.vector
        def _(dve):
            v = nc.vector

            def row_max(n, b):
                m = 2 * n + b
                dve.wait_ge(pe_s, m + 1)
                if m >= 2:
                    dve.wait_ge(d_s, m - 1)
                v.tensor_reduce(smax[:, b, :], ps_score[b][:, :].rearrange("q (p k) -> q p k", k=S),
                                AX.X, ALU.max).then_inc(d_mx, 1)

            def minus_max(n, b):
                m = 2 * n + b
                dve.wait_ge(d_mx, m + 1)
                if m >= 2:
                    dve.wait_ge(a_p, m - 1)
                v.tensor_tensor(s_sb[:, b, :].rearrange("q (p k) -> q p k", k=S),
                                ps_score[b][:, :].rearrange("q (p k) -> q p k", k=S),
                                smax[:, b, :].rearrange("q (p u) -> q p u", u=1).to_broadcast([P, NP, S]),
                                ALU.subtract).then_inc(d_s, 1)

            def copy_v(n):
                i = n % 2
                dve.wait_ge(pe_qkv, n + 1)
                if n == 0:
                    dve.wait_ge(c_zero, 6)
                if n >= 2:
                    dve.wait_ge(pe_o, 2 * (n - 1))
                for b in range(2):
                    for p2 in range(2):
                        v.tensor_copy(vbd[p2 * S:(p2 + 1) * S, i, b, :, p2, 0:16],
                                      ps_v[b * S:(b + 1) * S, :]
                                      .rearrange("k (j p c) -> k j p c", p=2, c=16)[:, :, p2, :]).then_inc(d_v, 1)

            def norm_o(n):
                i = n % 2
                dve.wait_ge(pe_o, 2 * (n + 1))
                if n >= 2:
                    dve.wait_ge(d_o, 2 * (n - 1))
                o = ps_o[:, 0:272].rearrange("q (b p c) -> q b p c", b=2, c=17)
                v.reciprocal(rsum[:, i, :].rearrange("q (b p u) -> q b p u", b=2, u=1),
                             o[:, :, :, 16:17]).then_inc(d_rs, 1)
                dve.wait_ge(d_rs, n + 1)
                if n >= 2:
                    dve.wait_ge(pe_ot, n - 1)
                for a in range(2):
                    q = slice(a * S, (a + 1) * S)
                    v.tensor_tensor(o_sb[q, i, :, :, a, :], o[q, :, :, a * HD:(a + 1) * HD],
                                    rsum[q, i, :].rearrange("q (b p u) -> q b p u", b=2, u=1)
                                    .to_broadcast([S, 2, NP, HD]), ALU.mult).then_inc(d_o, 1)

            def add_res(n):
                s, t, i = n // NT, n % NT, n % 2
                dve.wait_ge(pe_y, n + 1)
                if s < 2:
                    dve.wait_ge(c_resb, 1 if s == 0 else t + 2)
                    if n >= 2:
                        dve.wait_ge(d_x, n - 1)
                    v.tensor_tensor(res[:, i, :], ps_y[:, P:2 * P], res_b[:, s, t, :], ALU.add).then_inc(d_res, 1)
                    dve.wait_ge(d_res, n + 1)
                    v.bn_stats(stats[:, i, :], res[:, i, :]).then_inc(d_st, 1)
                    dve.wait_ge(d_st, n + 1)
                    if n >= 2:
                        dve.wait_ge(g_rs, cnt_rs(n - 2))
                    v.bn_aggr(mv[:, i, :], stats[:, i, :]).then_inc(d_mv, 1)
                else:
                    dve.wait_ge(d_x, NT + t + 1)
                    v.tensor_tensor(h3[:, t, :], ps_y[:, P:2 * P], x2[:, t, :], ALU.add).then_inc(d_res, 1)

            def finish(n):
                s, t, i = n // NT, n % NT, n % 2
                dve.wait_ge(g_rs, cnt_rs(n))
                if s < 2:
                    v.tensor_scalar((x1, x2)[s][:, t, :], res[:, i, :], mv[:, i, 0:1], rstd[:, i, 1:2],
                                    ALU.subtract, ALU.mult).then_inc(d_x, 1)
                if s == 1:
                    dve.wait_ge(d_x, n + 1)
                    if t == 0:
                        dve.wait_ge(c_rope, 2)
                    if t >= 1:
                        dve.wait_ge(d_xr, 2 * t)
                    for r, w in ((rope_a, rope_c), (rope_b, rope_s)):
                        v.scalar_tensor_tensor(r[:, :], x2[:, t, :], rstd[:, i, 3:4], w[:, :],
                                               ALU.mult, ALU.mult).then_inc(d_ra, 1)
                    dve.wait_ge(d_ra, 2 * (t + 1))
                    ra = rope_a[:, :].rearrange("q (h e) -> q h e", e=2)
                    rbb = rope_b[:, :].rearrange("q (h e) -> q h e", e=2)
                    half = D // 2
                    v.tensor_tensor(xr[:, t, 0:half], ra[:, :, 0], rbb[:, :, 1], ALU.subtract).then_inc(d_xr, 1)
                    v.tensor_tensor(xr[:, t, half:D], rbb[:, :, 0], ra[:, :, 1], ALU.add).then_inc(d_xr, 1)
                if s == 2:
                    v.scalar_tensor_tensor(xm[:, t, :], h3[:, t, :], rstd[:, i, 1:2], w_norm[:, 1, :],
                                           ALU.mult, ALU.mult).then_inc(d_xm, 1)

            v.memset(vbd[:, :, :, :, :, :], 0.0).then_inc(c_zero, 1)
            v.memset(o_sb[:, :, :, :, :, :], 0.0).then_inc(c_zero, 1)
            dve.wait_ge(c_zero, 2)
            v.memset(vbd[0:S, :, :, :, 0, 16:17], 1.0).then_inc(c_zero, 1)
            v.memset(vbd[S:P, :, :, :, 1, 16:17], 1.0).then_inc(c_zero, 1)
            v.memset(ones_bf[:, :], 1.0).then_inc(c_zero, 1)
            v.memset(bias_col[:, 2, :], 0.0).then_inc(c_zero, 1)
            for it in range(STEPS + 4):
                if it == 0:
                    copy_v(0)
                if it < STEPS:
                    row_max(it, 0)
                    minus_max(it, 0)
                if 3 <= it < STEPS + 3:
                    finish(it - 3)
                if it < STEPS:
                    row_max(it, 1)
                    minus_max(it, 1)
                if it + 1 < STEPS:
                    copy_v(it + 1)
                if 1 <= it <= STEPS:
                    norm_o(it - 1)
                if 2 <= it < STEPS + 2:
                    add_res(it - 2)

            chain = [0]

            def link(ins):
                chain[0] += 1
                ins.then_inc(d_rt, 1)
                dve.wait_ge(d_rt, chain[0])

            dve.wait_ge(pe_lg, NT)
            full = [P, NT, NE]
            lg = logit[:, :, :]

            def bc(ap):
                return ap.rearrange("q (t u) -> q t u", u=1).to_broadcast(full)

            dve.wait_ge(in_moe, MOE_LOADS)
            v.tensor_tensor(lg, ps_qkv[:, 0:NT * NE].rearrange("q (t e) -> q t e", e=NE), rb[:, :].rearrange("q (u e) -> q u e", u=1).to_broadcast(full),
                            ALU.add).then_inc(d_lg, 1)
            dve.wait_ge(d_lg, 1)
            order = rt[:, 7, :, :]
            for e in range(NE):
                k = v.memset(rt[:, 7, :, e:e + 1], float(NE - e))
            link(k)

            def pick(src, vmax, one_hot):
                link(v.tensor_reduce(vmax, src, AX.X, ALU.max))
                link(v.tensor_tensor(rt[:, 0, :, :], src, bc(vmax), ALU.is_equal))
                link(v.tensor_tensor(rt[:, 1, :, :], rt[:, 0, :, :], order, ALU.mult))
                link(v.tensor_reduce(rv[:, 7, :], rt[:, 1, :, :], AX.X, ALU.max))
                link(v.tensor_tensor(one_hot, rt[:, 1, :, :], bc(rv[:, 7, :]), ALU.is_equal))

            pick(lg, rv[:, 0, :], rt[:, 2, :, :])
            link(v.scalar_tensor_tensor(rt[:, 3, :, :], rt[:, 2, :, :], -3.0e38, lg, ALU.mult, ALU.add))
            pick(rt[:, 3, :, :], rv[:, 1, :], rt[:, 4, :, :])
            link(v.tensor_tensor(rv[:, 2, :], rv[:, 1, :], rv[:, 0, :], ALU.subtract))
            assert chain[0] == RT_EXP, chain
            dve.wait_ge(a_rt, 1)
            link(v.tensor_scalar(rv[:, 4, :], rv[:, 3, :], 1.0, None, ALU.add))
            link(v.reciprocal(rv[:, 5, :], rv[:, 4, :]))
            link(v.tensor_tensor(rv[:, 6, :], rv[:, 3, :], rv[:, 5, :], ALU.mult))
            link(v.tensor_tensor(rt[:, 5, :, :], rt[:, 2, :, :], bc(rv[:, 5, :]), ALU.mult))
            link(v.tensor_tensor(rt[:, 6, :, :], rt[:, 4, :, :], bc(rv[:, 6, :]), ALU.mult))
            link(v.tensor_tensor(comb[:, :, :], rt[:, 5, :, :], rt[:, 6, :, :], ALU.add))

            N = NT * NE
            for i in range(N + 2):
                if i < N:
                    dve.wait_ge(a_silu, i + 1)
                    if i >= 2:
                        dve.wait_ge(pe_ht, i - 1)
                    v.tensor_tensor(hh[:, i % 2, :], (bank[1], bank[3])[i % 2][:, :], silu[:, i % 2, :],
                                    ALU.mult).then_inc(d_hh, 1)
                if i >= 2:
                    j = i - 2
                    t, e = j // NE, j % NE
                    dve.wait_ge(pe_e, j + 1)
                    if j >= 1:
                        dve.wait_ge(d_acc, j)
                    src = base if e == 0 else acc
                    if e == 0:
                        dve.wait_ge(c_base, t + 1)
                    v.scalar_tensor_tensor(acc[:, t, :], (bank[5], bank[6])[j % 2][:, 0:D], comb[:, t, e:e + 1],
                                           src[:, t, :], ALU.mult, ALU.add).then_inc(d_acc, 1)

            dve.wait_ge(d_acc, N)
            for t in range(NT):
                v.bn_stats(fstats[:, t, :], acc[:, t, :]).then_inc(d_st, 1)
            for t in range(NT):
                dve.wait_ge(d_st, 2 * NT + t + 1)
                v.bn_aggr(fmv[:, t, :], fstats[:, t, :]).then_inc(d_fmv, 1)
            for t in range(NT):
                dve.wait_ge(g_frs, 2 * (t + 1))
                v.tensor_scalar(y_out[:, t, :], acc[:, t, :], fmv[:, t, 0:1], frstd[:, t, 1:2],
                                ALU.subtract, ALU.mult).then_inc(d_fin, 1)


def _consts():
    c = np.zeros((P, C_END), np.float32)
    r = np.arange(P)
    c[:, C_ID:C_ID + P] = np.eye(P)
    c[r, C_I2 + r % S] = 1
    q, k = r[:, None] % S, np.arange(512)[None, :] % S
    c[:, C_MASK:C_MASK + 512] = np.where(k <= q, 0.0, -1e30)
    half = P // 2
    theta = (np.float32(1.0) / np.float32(10000.0) ** (np.arange(half, dtype=np.float32) / np.float32(half)))
    ang = (r % S).astype(np.float32)[:, None] * theta[None, :].astype(np.float32)
    c[:, C_COS:C_COS + P] = np.repeat(np.cos(ang), 2, axis=1)
    c[:, C_SIN:C_SIN + P] = np.repeat(np.sin(ang), 2, axis=1)
    c[r, C_MA + (r // HD) % 2] = 1
    c[r, C_M8 + r // (2 * HD)] = 1
    return c


def kernel(**inputs):
    import concourse.bacc as bacc
    from concourse.bass_utils import run_bass_kernel_spmd

    nc = bacc.Bacc("TRN2", target_bir_lowering=False, num_devices=1)
    arrays, t_in = {}, {}
    for name, a in inputs.items():
        a = np.ascontiguousarray(a)
        arrays["in_" + name] = a
        t_in[name] = nc.dram_tensor("in_" + name, a.shape, mybir.dt.from_np(a.dtype), kind="ExternalInput").ap()
    arrays["in_consts"] = _consts()
    consts = nc.dram_tensor("in_consts", (P, C_END), F32, kind="ExternalInput").ap()
    out = nc.dram_tensor("out", (B, S, D), F32, kind="ExternalOutput").ap()
    decoder_kernel(nc, t_in, consts, out)
    r = run_bass_kernel_spmd(nc, [arrays], core_ids=[0])
    return r.results[0]["out"]
```

```python
from contextlib import ExitStack

import numpy as np

import concourse.bass as bass
from concourse import mybir

F32 = mybir.dt.float32
BF16 = mybir.dt.bfloat16
I32 = mybir.dt.int32
ALU = mybir.AluOpType
ACT = mybir.ActivationFunctionType
AX = mybir.AxisListType

P = 128
D = 128
S = 64
B = 16
NT = B * S // P
HD = 8
NP = 8
FF = 512
NE = 8
SCALE = float(HD) ** -0.5
STAGES = 3
STEPS = STAGES * NT
RT_EXP = 12
LN_EPS = 1e-5
RMS_EPS = 1e-6
NG = 26
NJ = 24
C_ID = 0
C_I2 = C_ID + P
C_MASK = C_I2 + S
C_COS = C_MASK + 512
C_SIN = C_COS + D
C_MA = C_SIN + D
C_M8 = C_MA + 2
C_IOTA = C_M8 + NP
C_TRI = C_IOTA + P
C_J = C_TRI + P
C_K = C_J + NG
C_LT = C_K + NE
C_P = C_LT + NE * NE
C_T = C_P + 1
C_ORD = C_T + 2 * NT
C_END = C_ORD + NE


def decoder_kernel(nc, t_in, consts, out):
    ctx = ExitStack()
    with ctx:
        def sb(name, shape, dt=F32):
            return ctx.enter_context(nc.sbuf_tensor(name, shape, dt))

        def sem(name):
            return ctx.enter_context(nc.semaphore(name))

        bank = [ctx.enter_context(nc.psum_tensor(f"bank{i}", [P, 512], F32)) for i in range(8)]
        ps_score = [bank[0], bank[1]]
        ps_pt = [bank[2], bank[3]]
        ps_xt, ps_qkv, ps_o, ps_y = bank[4], bank[5], bank[6], bank[7]
        ps_v = ps_xt[:, 2 * P:3 * P]

        cst = sb("cst", [P, C_END])
        ident = cst[:, C_ID:C_ID + P]
        fold2 = cst[:, C_I2:C_I2 + S]
        mask_a = cst[:, C_MA:C_MA + 2]
        mask_p = cst[:, C_M8:C_M8 + NP]
        ident_bf = sb("ident_bf", [P, P], BF16)
        mask_bf = sb("mask_bf", [P, 512], BF16)
        ones_bf = sb("ones_bf", [3, P], BF16)
        early = sb("early", [P, 4, NT, D])
        x_tok, c_tok, res_b = early[:, 0], early[:, 1], early[:, 2:4]
        xg = early[:, :].rearrange("q a t e -> q (a t) e")
        x1 = sb("x1", [P, NT, D])
        x2 = sb("x2", [P, NT, D])
        xr = sb("xr", [P, NT, D])
        h3 = sb("h3", [P, NT, D])
        w_raw = sb("w_raw", [P, 3 * D])
        wx_raw = sb("wx_raw", [P, 4, D])
        wkv_raw = sb("wkv_raw", [P, 2, 32])
        w_q = sb("w_q", [P, 3, D])
        w_k = sb("w_k", [P, 3, D])
        w_v = sb("w_v", [P, 3, D])
        w_o = sb("w_o", [P, 3, D])
        bias_col = sb("bias_col", [P, 3, 3])
        bias_qa = sb("bias_qa", [P, 3, 2])
        bias_row = sb("bias_row", [P, 2, D])
        w_norm = sb("w_norm", [P, 2, D])
        rope_c = sb("rope_c", [P, D])
        rope_s = sb("rope_s", [P, D])
        xt = sb("xt", [P, 2, 2, P])
        q2 = sb("q2", [P, 3, 2, 2, S])
        kt = sb("kt", [P, 2, P])
        k2 = sb("k2", [P, 3, 2, NP, S])
        vbd = sb("vbd", [P, 4, 2, 4, 2, 17])
        s_sb = sb("s_sb", [P, 2, 512])
        p_sb = sb("p_sb", [P, 2, 512])
        pt_sb = sb("pt_sb", [P, 2, 512])
        smax = sb("smax", [P, 2, NP])
        rsum = sb("rsum", [P, 2, 2 * NP])
        o_sb = sb("o_sb", [P, 2, 2, NP, 2, HD])
        ot_sb = sb("ot_sb", [P, 2, P])
        res = sb("res", [P, 2, D])
        stats = sb("stats", [P, 2, 6])
        mv = sb("mv", [P, 2, 2])
        rstd = sb("rstd", [P, 2, 4])
        half_neg = sb("half_neg", [P, 1])
        silu_first = sb("silu_first", [P, 1])
        all_in = sb("all_in", [P, 1])
        rope_a = sb("rope_a", [P, D])
        rope_b = sb("rope_b", [P, D])
        sq = sb("sq", [P, D])
        w1 = sb("w1", [P, NE, FF])
        w2 = sb("w2", [P, NE, FF])
        w3 = sb("w3", [P, NE, 4, D])
        rw = sb("rw", [P, NE])
        rb = sb("rb", [P, NE])
        b_raw = sb("b_raw", [NE, 2 * FF + D])
        b_hi = sb("b_hi", [NE, 2 * FF + D], BF16)
        b_mid = sb("b_mid", [NE, 2 * FF + D], BF16)
        b_lo = sb("b_lo", [NE, 2 * FF + D], BF16)
        b_row = sb("b_row", [3, NE, 2 * FF + D], BF16)
        xm = sb("xm", [P, NT, D])
        xmt = sb("xmt", [P, NT, D])
        logit = sb("logit", [P, NT, NE])
        rt = sb("rt", [P, 8, NT, NE])
        rv = sb("rv", [P, 8, NT])
        sel = sb("sel", [P, NT, NE], BF16)
        tri_bf = sb("tri_bf", [P, P], BF16)
        iota_bf = sb("iota_bf", [P, P], BF16)
        all1_bf = sb("all1_bf", [P, P], BF16)
        over = sb("over", [P, NE, NE])
        n_tiles = sb("n_tiles", [P, NE])
        first = sb("first", [P, NE])
        ex_f = sb("ex_f", [1, NJ, NE])
        ex_n = sb("ex_n", [1, NJ])
        quad_f = sb("quad_f", [1, 2, NJ // 2])
        quad_i = sb("quad_i", [1, NJ // 2], I32)
        last_i = sb("last_i", [1, 2], I32)
        dest = sb("dest", [P, NT, NE])
        slot_f = sb("slot_f", [P, 2, NT])
        slot_i = sb("slot_i", [P, 2, NT], I32)
        part_i = sb("part_i", [P, 2, 2 * NT], I32)
        part_f = sb("part_f", [P, 2, 2 * NT])
        lo_hot = sb("lo_hot", [P, 2 * NT, P], BF16)
        hi_hot = sb("hi_hot", [P, 2 * NT, NG])
        hi_p = sb("hi_p", [P, 2 * NT, NG], BF16)
        hi_t = sb("hi_t", [P, 2 * NT, NG], BF16)
        tok_i = sb("tok_i", [P, NG], I32)
        xs = sb("xs", [P, 2, P])
        xgt = sb("xgt", [P, 2, P])
        silu, hh, ht = s_sb, p_sb, pt_sb
        eo = sb("eo", [P, NJ, D])
        yg = k2[:, :, :, :, :].rearrange("q s b p k -> q (s b p k)")[:, 0:2 * NT * D].rearrange(
            "q (c e) -> q c e", e=D)
        acc = xr
        fstats = sb("fstats", [P, NT, 6])
        fmv = sb("fmv", [P, NT, 2])
        frstd = sb("frstd", [P, NT, 2])
        base = x2
        y_out = x1

        in_cst = sem("in_cst")
        in_x = sem("in_x")
        in_ctx = sem("in_ctx")
        in_w = sem("in_w")
        in_wx = sem("in_wx")
        in_b = sem("in_b")
        in_w3rd = sem("in_w3rd")
        in_moe = sem("in_moe")
        in_brow = sem("in_brow")
        out_done = sem("out_done")
        c_base = sem("c_base")
        c_bf = sem("c_bf")
        c_wq = sem("c_wq")
        c_wkv = sem("c_wkv")
        c_zero = sem("c_zero")
        c_bqa = sem("c_bqa")
        c_rope = sem("c_rope")
        c_resb = sem("c_resb")
        c_bparts = sem("c_bparts")
        c_half = sem("c_half")
        c_hot = sem("c_hot")
        pe_wx = sem("pe_wx")
        pe_xt = sem("pe_xt")
        pe_qkv = sem("pe_qkv")
        pe_s = sem("pe_s")
        pe_pt = sem("pe_pt")
        pe_o = sem("pe_o")
        pe_ot = sem("pe_ot")
        pe_y = sem("pe_y")
        a_wx = sem("a_wx")
        a_xt = sem("a_xt")
        a_q = sem("a_q")
        a_k = sem("a_k")
        a_p = sem("a_p")
        a_pt = sem("a_pt")
        a_ot = sem("a_ot")
        a_sq = sem("a_sq")
        d_mx = sem("d_mx")
        d_s = sem("d_s")
        d_v = sem("d_v")
        d_rs = sem("d_rs")
        d_o = sem("d_o")
        d_res = sem("d_res")
        d_st = sem("d_st")
        d_mv = sem("d_mv")
        d_x = sem("d_x")
        d_ra = sem("d_ra")
        d_xr = sem("d_xr")
        d_xm = sem("d_xm")
        g_k2 = sem("g_k2")
        g_rs = sem("g_rs")
        g_rq = sem("g_rq")
        d_fmv = sem("d_fmv")
        g_feps = sem("g_feps")
        g_frs = sem("g_frs")
        pe_rt_turn = sem("pe_rt_turn")
        a_rt_copy = sem("a_rt_copy")
        pe_lg = sem("pe_lg")
        d_lg = sem("d_lg")
        d_rt = sem("d_rt")
        a_rt = sem("a_rt")
        pe_rank = sem("pe_rank")
        pe_tok = sem("pe_tok")
        d_sel = sem("d_sel")
        d_ex = sem("d_ex")
        d_xs = sem("d_xs")
        d_hot = sem("d_hot")
        d_tok = sem("d_tok")
        xm_out = sem("xm_out")
        y_zero = sem("y_zero")
        y_out_s = sem("y_out_s")
        g_all = sem("g_all")
        g_gather = sem("g_gather")
        g_yg = [sem(f"g_yg{t}") for t in range(NT)]
        pe_xgt = sem("pe_xgt")
        a_xgt = sem("a_xgt")
        pe_h = sem("pe_h")
        a_silu = sem("a_silu")
        d_hh = sem("d_hh")
        pe_ht = sem("pe_ht")
        a_ht = sem("a_ht")
        pe_e = sem("pe_e")
        d_eo = sem("d_eo")
        d_fin = sem("d_fin")

        xm_d = nc.dram_tensor("xm_scratch", (NT * P, D), F32, kind="Internal").ap()
        y_d = nc.dram_tensor("y_scratch", (NJ * P, D), F32, kind="Internal").ap()

        block = ctx.enter_context(nc.Block())

        def rstd_sum(n):
            return mv[:, n % 2, 0:1]

        def cnt_rs(n):
            return n + 1 if n < NT else (NT + 2 * (n - NT + 1) if n < 2 * NT else 3 * NT + (n - 2 * NT + 1))

        @block.sync
        def _(sp):
            tiles = "(t c) s e -> (c s) t e"
            sp.dma_start(x_tok[:, :, :], t_in["x"].rearrange(tiles, c=2)).then_inc(in_x, 16)
            sp.dma_start(w_raw[:, :], t_in["L0_attn_W1"]).then_inc(in_w, 16)
            sp.dma_start(w_o[:, 0, :], t_in["L0_attn_W2"]).then_inc(in_w, 16)
            b1 = t_in["L0_attn_b1"].rearrange("(h c d) -> c h d", c=3, d=HD)
            for c in range(3):
                sp.dma_start(bias_col[:, 0, c:c + 1], b1[c].rearrange("h (d u) -> h d u", u=1)).then_inc(in_b, 16)
            for c, n in enumerate(("bq", "bk", "bv")):
                sp.dma_start(bias_col[:, 1, c:c + 1],
                             t_in["L0_xattn_" + n].rearrange("(d u) -> d u", u=1)).then_inc(in_b, 16)
            for r, n in ((bias_row[:, 0, :], "L0_attn_b2"), (bias_row[:, 1, :], "L0_xattn_bo"),
                         (w_norm[:, 0, :], "L0_ffn_norm1_w"), (w_norm[:, 1, :], "L0_ffn_norm2_w")):
                sp.dma_start(r, t_in[n].rearrange("(a e) -> a e", a=1).to_broadcast([P, D])).then_inc(in_w3rd, 16)
            sp.dma_start(w_q[:, 2, :], t_in["L0_ffn_Wq"]).then_inc(in_w3rd, 16)
            sp.dma_start(w_o[:, 2, :], t_in["L0_ffn_Wo"]).then_inc(in_w3rd, 16)
            sp.dma_start(wkv_raw[:, 0, :], t_in["L0_ffn_Wk"]).then_inc(in_w3rd, 16)
            sp.dma_start(wkv_raw[:, 1, :], t_in["L0_ffn_Wv"]).then_inc(in_w3rd, 16)
            sp.dma_start(b_raw[:, 0:FF], t_in["L0_ffn_b1"]).then_inc(in_w3rd, 16)
            sp.dma_start(b_raw[:, FF:2 * FF], t_in["L0_ffn_b2"]).then_inc(in_w3rd, 16)
            sp.dma_start(b_raw[:, 2 * FF:], t_in["L0_ffn_b3"]).then_inc(in_w3rd, 16)
            sp.dma_start(c_tok[:, :, :], t_in["ctx_1024"].rearrange(tiles, c=2)).then_inc(in_ctx, 16)
            sp.dma_start(w1[:, :, :], t_in["L0_ffn_W1"].rearrange("e d f -> d e f")).then_inc(in_moe, 16)
            sp.dma_start(w2[:, :, :], t_in["L0_ffn_W2"].rearrange("e d f -> d e f")).then_inc(in_moe, 16)
            for e in range(NE):
                sp.dma_start(w3[:, e, :, :],
                             t_in["L0_ffn_W3"][e].rearrange("(c f) d -> f c d", f=P)).then_inc(in_moe, 16)
            sp.dma_start(rw[:, :], t_in["L0_ffn_router_w"]).then_inc(in_moe, 16)
            sp.dma_start(rb[:, :], t_in["L0_ffn_router_b"].rearrange("(a e) -> a e", a=1)
                         .to_broadcast([P, NE])).then_inc(in_moe, 16)
            sp.wait_ge(c_bparts, 5)
            for k, part in enumerate((b_hi, b_mid, b_lo)):
                sp.dma_start(b_row[k:k + 1, :, :], part[:, :]).then_inc(in_brow, 16)
            sp.wait_ge(c_zero, 7)
            sp.dma_start(y_d.rearrange("(a q) e -> q a e", q=P), eo[:, :, :]).then_inc(y_zero, 16)
            for t in range(NT):
                sp.wait_ge(d_xm, t + 1)
                sp.dma_start(xm_d[t * P:(t + 1) * P, :], xm[:, t, :]).then_inc(xm_out, 16)
            sp.wait_ge(y_zero, 16)
            sp.wait_ge(d_ex, 1)
            last = sp.value_load(last_i[0:1, 0:1], min_val=NT - 1, max_val=NJ // 2 - 1)
            with sp.Fori(0, last + 1) as i:
                sp.wait_ge(d_eo, 2 * i + 2)
                sp.dma_start(y_d.rearrange("(a q) e -> q a e", q=P)[:, bass.ds(i * 2, 2), :],
                             eo[:, bass.ds(i * 2, 2), :]).then_inc(y_out_s, 16)
            for t in range(NT):
                sp.wait_ge(d_fin, t + 1)
                sp.dma_start(out.rearrange(tiles, c=2)[:, t, :], y_out[:, t, :]).then_inc(out_done, 16)
            sp.wait_ge(out_done, 16 * NT)

        MOE_LOADS = 16 * (2 + NE + 2)

        @block.gpsimd
        def _(pool):
            g = nc.gpsimd
            g.memset(half_neg[:, :], -0.5).then_inc(c_half, 1)
            pool.wait_ge(in_cst, 16)
            pool.wait_ge(in_b, 96)
            pool.wait_ge(c_zero, 6)
            for s in range(3):
                for a in range(2):
                    g.tensor_tensor(bias_qa[:, s, a:a + 1], bias_col[:, s, 0:1], mask_a[:, a:a + 1],
                                    ALU.mult).then_inc(c_bqa, 1)
            def first_residual():
                pool.wait_ge(in_x, 16)
                pool.wait_ge(in_w3rd, 16 * 11)
                g.tensor_tensor(res_b[:, 0, :, :], x_tok[:, :, :],
                                bias_row[:, 0:1, :].to_broadcast([P, NT, D]), ALU.add).then_inc(c_resb, 1)

            def late_setup(i):
                if i < 2:
                    r, c = ((rope_c, C_COS), (rope_s, C_SIN))[i]
                    g.tensor_tensor(r[:, :], cst[:, c:c + D], w_norm[:, 0, :], ALU.mult).then_inc(c_rope, 1)
                elif i < 4:
                    g.tensor_copy((w_k, w_v)[i - 2][:, 2, :].rearrange("e (g r d) -> e g r d", r=4, d=HD),
                                  wkv_raw[:, i - 2, :].rearrange("e (g u d) -> e g u d", u=1, d=HD)
                                  .to_broadcast([P, 4, 4, HD])).then_inc(c_wkv, 1)
                else:
                    if i > 4:
                        pool.wait_ge(c_bparts, i - 4)
                    part = (b_hi, b_mid, b_lo)[(i - 4) // 2]
                    if i % 2 == 0:
                        g.tensor_copy(part[:, :], b_raw[:, :]).then_inc(c_bparts, 1)
                    else:
                        g.tensor_tensor(b_raw[:, :], b_raw[:, :], part[:, :], ALU.subtract).then_inc(c_bparts, 1)

            def expand_keys(n):
                pool.wait_ge(a_k, n + 1)
                if n >= 3:
                    pool.wait_ge(pe_s, 2 * (n - 2))
                g.tensor_tensor(
                    k2[:, n % 3, :, :, :],
                    kt[:, n % 2, :].rearrange("c (b u k) -> c b u k", b=2, u=1).to_broadcast([P, 2, NP, S]),
                    mask_p.rearrange("c (v p u) -> c v p u", v=1, u=1).to_broadcast([P, 2, NP, S]),
                    ALU.mult).then_inc(g_k2, 1)

            links = [0]

            def link():
                links[0] += 1
                pool.wait_ge(g_rq, links[0])

            def row_scale(n):
                s, i = n // NT, n % 2
                r = rstd[:, i, :]
                if s < 2:
                    pool.wait_ge(d_mv, n + 1)
                    if n >= 2:
                        pool.wait_ge(d_x, n - 1)
                        if n - 2 >= NT:
                            pool.wait_ge(d_ra, 2 * (n - 2 - NT + 1))
                    g.tensor_scalar(r[:, 0:1], mv[:, i, 1:2], LN_EPS, None, ALU.add).then_inc(g_rq, 1)
                    link()
                    g.tensor_tensor(r[:, 1:2], r[:, 0:1], half_neg[:, :], ALU.pow).then_inc(g_rs, 1)
                    if s == 1:
                        pool.wait_ge(g_rs, cnt_rs(n) - 1)
                        g.tensor_tensor(r[:, 2:3], r[:, 1:2], r[:, 1:2], ALU.mult).then_inc(g_rq, 1)
                        link()
                        g.tensor_tensor(r[:, 2:3], r[:, 2:3], mv[:, i, 1:2], ALU.mult).then_inc(g_rq, 1)
                        link()
                        g.tensor_scalar(r[:, 2:3], r[:, 2:3], RMS_EPS, None, ALU.add).then_inc(g_rq, 1)
                        link()
                        g.tensor_tensor(r[:, 3:4], r[:, 2:3], half_neg[:, :], ALU.pow).then_inc(g_rs, 1)
                else:
                    pool.wait_ge(a_sq, n - 2 * NT + 1)
                    pool.wait_ge(d_ra, 2 * NT)
                    if n - 2 >= 2 * NT:
                        pool.wait_ge(d_xm, n - 2 - 2 * NT + 1)
                    g.tensor_scalar(r[:, 0:1], rstd_sum(n), 1.0 / D, RMS_EPS, ALU.mult, ALU.add).then_inc(g_rq, 1)
                    link()
                    g.tensor_tensor(r[:, 1:2], r[:, 0:1], half_neg[:, :], ALU.pow).then_inc(g_rs, 1)

            def add_bias(n):
                if n < NT:
                    pool.wait_ge(d_x, n + 1)
                    g.tensor_tensor(res_b[:, 1, n, :], x1[:, n, :], bias_row[:, 1, :], ALU.add).then_inc(c_resb, 1)

            def last_scale(a, b):
                pool.wait_ge(d_fmv, b)
                g.tensor_scalar(frstd[:, a:b, 0], fmv[:, a:b, 1], LN_EPS, None, ALU.add).then_inc(g_feps, 1)
                pool.wait_ge(g_feps, 1 if a == 0 else 2)
                g.tensor_tensor(frstd[:, a:b, 1], frstd[:, a:b, 0], half_neg[:, :].to_broadcast([P, b - a]),
                                ALU.pow).then_inc(g_frs, 1)

            expand_keys(0)
            expand_keys(1)
            first_residual()
            for it in range(STEPS + 3):
                if it >= 3:
                    row_scale(it - 3)
                if it + 2 < STEPS:
                    expand_keys(it + 2)
                if it >= 4:
                    add_bias(it - 4)
                if 3 <= it < 12:
                    late_setup(it - 3)
            for t in range(NT):
                pool.wait_ge(d_res, 2 * NT + t + 1)
                g.tensor_tensor(base[:, t, :], h3[:, t, :], x2[:, t, :], ALU.add).then_inc(c_base, 1)
            pool.wait_ge(xm_out, 16 * NT)
            pool.wait_ge(d_tok, 1)
            for j in range(NG):
                pool.indirect_dma_start(xg[:, j, :], None, xm_d[:, :],
                                        bass.IndirectOffsetOnAxis(ap=tok_i[:, j:j + 1], axis=0)).then_inc(g_gather, 16)
                if j % 2 == 1:
                    pool.wait_ge(g_gather, 16 * (j + 1))
            pool.wait_ge(d_ex, 1)
            last = pool.value_load(last_i[0:1, 0:1], min_val=NT - 1, max_val=NJ // 2 - 1)
            pool.wait_ge(y_out_s, last * 16 + 16)
            g.tensor_tensor(all_in[:, :], half_neg[:, :], half_neg[:, :], ALU.mult).then_inc(g_all, 1)
            pool.wait_ge(g_all, 1)
            for t in range(NT):
                for k in range(2):
                    pool.indirect_dma_start(yg[:, 2 * t + k, :], None, y_d[:, :],
                                            bass.IndirectOffsetOnAxis(ap=slot_i[:, k, t:t + 1], axis=0)).then_inc(g_yg[t], 16)
            last_scale(0, NT - 1)
            last_scale(NT - 1, NT)

        @block.tensor
        def _(pe):
            mm = nc.tensor.matmul

            def turn(o, i, idn):
                return mm(o, i, idn, start=True, stop=True, is_transpose=True)

            def turn_x(n):
                s, t = n // NT, n % NT
                if s == 0:
                    pe.wait_ge(in_x, 16)
                elif s == 1:
                    pe.wait_ge(d_x, t + 1)
                    pe.wait_ge(in_ctx, 16)
                else:
                    pe.wait_ge(d_xr, 2 * (t + 1))
                if n >= 1:
                    pe.wait_ge(a_xt, n)
                    pe.wait_ge(d_v, 4 * n)
                src = (x_tok, x1, xr)[s]
                m = turn(ps_xt[:, 0:P], src[:, t, :], ident)
                if s == 1:
                    m = turn(ps_xt[:, P:2 * P], c_tok[:, t, :], ident)
                m.then_inc(pe_xt, 1)

            def project(n):
                s, i = n // NT, n % 2
                pe.wait_ge(a_xt, n + 1)
                if n >= 1:
                    pe.wait_ge(a_q, 2 * n)
                    pe.wait_ge(a_k, n)
                    pe.wait_ge(d_v, 4 * n)
                if n == 0:
                    pe.wait_ge(c_wq, 3)
                if n == NT:
                    pe.wait_ge(a_wx, 1)
                if n == 2 * NT:
                    pe.wait_ge(c_wkv, 2)
                kv = xt[:, i, 1 if s == 1 else 0, :]
                mm(ps_qkv[:, 0:P], w_q[:, s, :], xt[:, i, 0, :], start=True, stop=True)
                mm(ps_qkv[:, P:2 * P], w_k[:, s, :], kv, start=True, stop=True)
                mm(ps_v, kv, w_v[:, s, :], start=True, stop=True).then_inc(pe_qkv, 1)

            def scores(n, b):
                m, i = 2 * n + b, n % 3
                if b == 0:
                    pe.wait_ge(a_q, 2 * (n + 1))
                    pe.wait_ge(g_k2, n + 1)
                if m >= 2:
                    pe.wait_ge(d_s, m - 1)
                mm(ps_score[b][:, :], ident_bf[:, :], mask_bf[:, :], start=True, stop=False)
                mm(ps_score[b][:, :], q2[:, i, b, :, :].rearrange("c a q -> c (a q)"),
                   k2[:, i, b, :, :].rearrange("c p k -> c (p k)"), start=False, stop=True).then_inc(pe_s, 1)

            def turn_p(n, b):
                m = 2 * n + b
                pe.wait_ge(a_p, m + 1)
                if m >= 2:
                    pe.wait_ge(a_pt, m - 1)
                for j in range(4):
                    k = turn(ps_pt[b][:, j * P:(j + 1) * P], p_sb[:, b, j * P:(j + 1) * P], ident)
                k.then_inc(pe_pt, 1)

            def values(n, b):
                m, i = 2 * n + b, n % 4
                pe.wait_ge(a_pt, m + 1)
                if b == 0:
                    pe.wait_ge(d_v, 4 * (n + 1))
                    if n >= 1:
                        pe.wait_ge(d_o, 2 * n)
                for j in range(4):
                    c = b * 136 + j * 34
                    k = mm(ps_o[:, c:c + 34], pt_sb[:, b, j * P:(j + 1) * P],
                           vbd[:, i, b, j, :, :].rearrange("k p c -> k (p c)"), start=True, stop=True)
                k.then_inc(pe_o, 1)

            def turn_o(n):
                i = n % 2
                pe.wait_ge(d_o, 2 * (n + 1))
                if n >= 1:
                    pe.wait_ge(d_res, n)
                for b in range(2):
                    k = mm(ps_y[:, b * S:(b + 1) * S], o_sb[:, i, b, :, :, :].rearrange("q p a d -> q (p a d)"),
                           fold2, start=True, stop=True)
                k.then_inc(pe_ot, 1)

            def out_proj(n):
                s, i = n // NT, n % 2
                pe.wait_ge(a_ot, n + 1)
                mm(ps_y[:, P:2 * P], ot_sb[:, i, :], w_o[:, s, :], start=True, stop=True).then_inc(pe_y, 1)

            def route_turn(h):
                for t in range(4 * h, 4 * h + 4):
                    pe.wait_ge(d_xm, t + 1)
                    k = turn(ps_pt[h][:, (t % 4) * P:(t % 4 + 1) * P], xm[:, t, :], ident)
                k.then_inc(pe_rt_turn, 1)

            def route_logits(h):
                pe.wait_ge(a_rt_copy, h + 1)
                pe.wait_ge(in_moe, MOE_LOADS)
                for t in range(4 * h, 4 * h + 4):
                    k = mm(ps_qkv[:, t * NE:(t + 1) * NE], xmt[:, t, :], rw[:, :], start=True, stop=True)
                k.then_inc(pe_lg, 1)

            pe.wait_ge(in_cst, 16)
            turn_x(0)
            project(0)
            pe.wait_ge(in_wx, 64)
            for c in range(4):
                k = turn(ps_pt[0][:, c * P:(c + 1) * P], wx_raw[:, c, :], ident)
            k.then_inc(pe_wx, 1)
            pe.wait_ge(a_wx, 1)
            turn_x(1)
            project(1)
            pe.wait_ge(c_bf, 2)
            for it in range(STEPS + 2):
                if it < STEPS:
                    scores(it, 0)
                    scores(it, 1)
                if it + 2 < STEPS:
                    turn_x(it + 2)
                if 1 <= it <= STEPS:
                    turn_p(it - 1, 0)
                    turn_p(it - 1, 1)
                if it + 2 < STEPS:
                    project(it + 2)
                if 2 <= it:
                    turn_o(it - 2)
                if 1 <= it <= STEPS:
                    values(it - 1, 0)
                    values(it - 1, 1)
                if 2 <= it:
                    out_proj(it - 2)
                if it == STEPS:
                    route_turn(0)

            route_turn(1)
            route_logits(0)
            route_logits(1)

            ps_rank, ps_count, ps_tok = bank[6][:, 0:NT * NE], bank[6][:, NT * NE:NT * NE + NE], bank[7][:, 0:NG]
            pe.wait_ge(d_sel, 1)
            pe.wait_ge(c_hot, 3)
            mm(ps_rank, tri_bf[:, :], sel[:, :, :].rearrange("q t e -> q (t e)"), start=True, stop=False)
            for t in range(NT - 1):
                u = NT - 1 - t
                mm(bank[6][:, (t + 1) * NE:NT * NE], all1_bf[:, :],
                   sel[:, t:t + 1, :].to_broadcast([P, u, NE]), start=False, stop=(t == NT - 2))
            for t in range(NT):
                k = mm(ps_count, all1_bf[:, :], sel[:, t, :], start=(t == 0), stop=(t == NT - 1))
            k.then_inc(pe_rank, 1)
            pe.wait_ge(d_hot, 2)
            for c in range(2 * NT):
                pe.wait_ge(d_hot, 3 + c)
                mm(ps_tok, lo_hot[:, c, :], hi_p[:, c, :], start=(c == 0), stop=False)
                k = mm(ps_tok, lo_hot[:, c, :], hi_t[:, c, :], start=False, stop=(c == 2 * NT - 1))
            k.then_inc(pe_tok, 1)

            ps_h1, ps_h2 = [bank[0], bank[2]], [bank[1], bank[3]]
            ps_ht, ps_e, ps_xgt = bank[4], [bank[5], bank[6]], bank[7]

            def turn_slots():
                for u in range(2):
                    k = turn(ps_xgt[:, u * P:(u + 1) * P], xs[:, u, :], ident)
                k.then_inc(pe_xgt, 1)

            def up(u, e):
                for dst, w, c in ((ps_h1, w1, 0), (ps_h2, w2, FF)):
                    mm(dst[u][:, :], xgt[:, u, :], w[:, bass.ds(e, 1), :].rearrange("d a f -> d (a f)"),
                       start=True, stop=False)
                    mm(dst[u][:, :], ones_bf[:, :],
                       b_row[:, bass.ds(e, 1), c:c + FF].rearrange("d a f -> d (a f)"),
                       start=False, stop=True).then_inc(pe_h, 1)

            def turn_h(u):
                for c in range(4):
                    k = turn(ps_ht[:, c * P:(c + 1) * P], hh[:, u, c * P:(c + 1) * P], ident)
                k.then_inc(pe_ht, 1)

            def down(u, e):
                dst = ps_e[u][:, 0:D]
                for c in range(4):
                    mm(dst, ht[:, u, c * P:(c + 1) * P], w3[:, bass.ds(e, 1), c, :].rearrange("d a f -> d (a f)"),
                       start=(c == 0), stop=False)
                mm(dst, ones_bf[:, :], b_row[:, bass.ds(e, 1), 2 * FF:2 * FF + D].rearrange("d a f -> d (a f)"),
                   start=False, stop=True).then_inc(pe_e, 1)

            def experts_of(i):
                w = pe.value_load(quad_i[0:1, bass.ds(i, 1)], min_val=0, max_val=NE ** 4 - 1)
                return tuple(pe.snap((w >> 3 * k) & 7) for k in range(4))

            pe.wait_ge(in_brow, 48)
            pe.wait_ge(in_moe, MOE_LOADS)
            pe.wait_ge(d_ex, 1)
            pe.wait_ge(d_tok, 1)
            ea, eb, _, _ = experts_of(0)
            last = pe.value_load(last_i[0:1, 0:1], min_val=NT - 1, max_val=NJ // 2 - 1)
            pe.wait_ge(d_xs, 1)
            turn_slots()
            pe.wait_ge(a_xgt, 2)
            up(0, ea)
            pe.wait_ge(d_xs, 2)
            turn_slots()
            up(1, eb)
            pe.wait_ge(d_hh, 1)
            turn_h(0)
            with pe.Fori(0, last) as i:
                before_a, before_b, ea, eb = experts_of(i)
                pe.wait_ge(a_xgt, 2 * i + 3)
                up(0, ea)
                pe.wait_ge(d_hh, 2 * i + 2)
                pe.wait_ge(a_ht, 2 * i + 1)
                turn_h(1)
                pe.wait_ge(d_xs, i + 3)
                pe.wait_ge(a_xgt, 2 * i + 4)
                turn_slots()
                down(0, before_a)
                up(1, eb)
                pe.wait_ge(a_ht, 2 * i + 2)
                down(1, before_b)
                pe.wait_ge(d_hh, 2 * i + 3)
                turn_h(0)
            _, _, ea, eb = experts_of(last - 1)
            pe.wait_ge(d_hh, 2 * last + 2)
            pe.wait_ge(a_ht, 2 * last + 1)
            turn_h(1)
            down(0, ea)
            pe.wait_ge(a_ht, 2 * last + 2)
            down(1, eb)

        @block.scalar
        def _(act):
            A = nc.scalar.activation
            act.dma_start(cst[:, :], consts).then_inc(in_cst, 16)
            for c, n in enumerate(("wq", "wk", "wv", "wo")):
                act.dma_start(wx_raw[:, c, :], t_in["L0_xattn_" + n]).then_inc(in_wx, 16)

            def copy_xt(n):
                act.wait_ge(pe_xt, n + 1)
                if n >= 2:
                    act.wait_ge(pe_qkv, n - 1)
                w = 2 if n // NT == 1 else 1
                A(xt[:, n % 2, 0:w, :].rearrange("c x t -> c (x t)"), ps_xt[:, 0:w * P], ACT.Copy).then_inc(a_xt, 1)

            def copy_qk(n):
                s, i = n // NT, n % 2
                act.wait_ge(pe_qkv, n + 1)
                if n == 0:
                    act.wait_ge(c_bqa, 6)
                if n >= 2:
                    act.wait_ge(g_k2, n - 1)
                if n >= 3:
                    act.wait_ge(pe_s, 2 * (n - 2))
                A(kt[:, i, :], ps_qkv[:, P:2 * P], ACT.Identity, bias=bias_col[:, s, 1:2]).then_inc(a_k, 1)
                for a in range(2):
                    A(q2[:, n % 3, :, a, :], ps_qkv[:, 0:P].rearrange("c (b q) -> c b q", b=2), ACT.Identity,
                      bias=bias_qa[:, s, a:a + 1], scale=mask_a[:, a:a + 1]).then_inc(a_q, 1)

            def exponent(n, b):
                m = 2 * n + b
                act.wait_ge(d_s, m + 1)
                if m >= 2:
                    act.wait_ge(pe_pt, m - 1)
                A(p_sb[:, b, :], s_sb[:, b, :], ACT.Exp, scale=SCALE).then_inc(a_p, 1)

            def copy_pt(n, b):
                m = 2 * n + b
                act.wait_ge(pe_pt, m + 1)
                if m >= 2:
                    act.wait_ge(pe_o, m - 1)
                A(pt_sb[:, b, :], ps_pt[b][:, :], ACT.Copy).then_inc(a_pt, 1)

            def copy_ot(n):
                s = n // NT
                act.wait_ge(pe_ot, n + 1)
                if n >= 2:
                    act.wait_ge(pe_y, n - 1)
                A(ot_sb[:, n % 2, :], ps_y[:, 0:P], ACT.Identity, bias=bias_col[:, s, 2:3]).then_inc(a_ot, 1)

            def square(n):
                t = n - 2 * NT
                act.wait_ge(d_res, n + 1)
                if t >= 1:
                    act.wait_ge(a_sq, t)
                if t >= 2:
                    act.wait_ge(g_rs, cnt_rs(n - 2))
                A(sq[:, :], h3[:, t, :], ACT.Square, accum_out=mv[:, n % 2, 0:1]).then_inc(a_sq, 1)

            copy_xt(0)
            act.wait_ge(in_cst, 16)
            copy_qk(0)
            act.wait_ge(pe_wx, 1)
            for c, w in enumerate((w_q, w_k, w_v, w_o)):
                k = A(w[:, 1, :], ps_pt[0][:, c * P:(c + 1) * P], ACT.Copy)
            k.then_inc(a_wx, 1)
            copy_xt(1)
            copy_qk(1)
            for it in range(STEPS + 3):
                if it - 3 >= 2 * NT:
                    square(it - 3)
                if it + 2 < STEPS:
                    copy_xt(it + 2)
                if it < STEPS:
                    exponent(it, 0)
                if 1 <= it <= STEPS:
                    copy_pt(it - 1, 0)
                    copy_pt(it - 1, 1)
                if it < STEPS:
                    exponent(it, 1)
                if 2 <= it < STEPS + 2:
                    copy_ot(it - 2)
                if it + 2 < STEPS:
                    copy_qk(it + 2)
            for h in range(2):
                act.wait_ge(pe_rt_turn, h + 1)
                A(xmt[:, 4 * h:4 * h + 4, :].rearrange("c t q -> c (t q)"), ps_pt[h][:, :], ACT.Copy).then_inc(a_rt_copy, 1)
            act.wait_ge(d_rt, RT_EXP)
            A(rv[:, 3, :], rv[:, 2, :], ACT.Exp).then_inc(a_rt, 1)
            act.wait_ge(c_half, 1)
            A(silu_first[:, :], half_neg[:, :], ACT.Silu)

            ps_h1 = [bank[0], bank[2]]

            def copy_slots(u):
                A(xgt[:, u, :], bank[7][:, u * P:(u + 1) * P], ACT.Copy).then_inc(a_xgt, 1)

            def gate(u):
                A(silu[:, u, :], ps_h1[u][:, :], ACT.Silu).then_inc(a_silu, 1)

            def copy_ht(u):
                A(ht[:, u, :], bank[4][:, :], ACT.Copy).then_inc(a_ht, 1)

            act.wait_ge(pe_xgt, 1)
            copy_slots(0)
            copy_slots(1)
            act.wait_ge(pe_h, 1)
            gate(0)
            act.wait_ge(pe_xgt, 2)
            act.wait_ge(pe_h, 2)
            copy_slots(0)
            act.wait_ge(pe_h, 3)
            gate(1)
            act.wait_ge(pe_h, 4)
            copy_slots(1)
            act.wait_ge(pe_ht, 1)
            copy_ht(0)
            act.wait_ge(d_ex, 1)
            last = act.value_load(last_i[0:1, 0:1], min_val=NT - 1, max_val=NJ // 2 - 1)
            with act.Fori(0, last) as i:
                act.wait_ge(pe_h, 4 * i + 5)
                act.wait_ge(d_hh, 2 * i + 1)
                gate(0)
                act.wait_ge(pe_ht, 2 * i + 2)
                copy_ht(1)
                act.wait_ge(pe_xgt, i + 3)
                copy_slots(0)
                act.wait_ge(pe_h, 4 * i + 7)
                act.wait_ge(d_hh, 2 * i + 2)
                gate(1)
                act.wait_ge(pe_h, 4 * i + 8)
                copy_slots(1)
                act.wait_ge(pe_ht, 2 * i + 3)
                copy_ht(0)
            act.wait_ge(pe_ht, 2 * last + 2)
            copy_ht(1)

        @block.vector
        def _(dve):
            v = nc.vector

            def row_max(n, b):
                m = 2 * n + b
                dve.wait_ge(pe_s, m + 1)
                if m >= 2:
                    dve.wait_ge(d_s, m - 1)
                v.tensor_reduce(smax[:, b, :], ps_score[b][:, :].rearrange("q (p k) -> q p k", k=S),
                                AX.X, ALU.max).then_inc(d_mx, 1)

            def minus_max(n, b):
                m = 2 * n + b
                dve.wait_ge(d_mx, m + 1)
                if m >= 2:
                    dve.wait_ge(a_p, m - 1)
                v.tensor_tensor(s_sb[:, b, :].rearrange("q (p k) -> q p k", k=S),
                                ps_score[b][:, :].rearrange("q (p k) -> q p k", k=S),
                                smax[:, b, :].rearrange("q (p u) -> q p u", u=1).to_broadcast([P, NP, S]),
                                ALU.subtract).then_inc(d_s, 1)

            def copy_v(n):
                i = n % 4
                dve.wait_ge(pe_qkv, n + 1)
                if n == 0:
                    dve.wait_ge(c_zero, 6)
                if n >= 4:
                    dve.wait_ge(pe_o, 2 * (n - 3))
                for b in range(2):
                    for p2 in range(2):
                        v.tensor_copy(vbd[p2 * S:(p2 + 1) * S, i, b, :, p2, 0:16],
                                      ps_v[b * S:(b + 1) * S, :]
                                      .rearrange("k (j p c) -> k j p c", p=2, c=16)[:, :, p2, :]).then_inc(d_v, 1)

            def norm_o(n):
                i = n % 2
                dve.wait_ge(pe_o, 2 * (n + 1))
                if n >= 2:
                    dve.wait_ge(d_o, 2 * (n - 1))
                o = ps_o[:, 0:272].rearrange("q (b p c) -> q b p c", b=2, c=17)
                v.reciprocal(rsum[:, i, :].rearrange("q (b p u) -> q b p u", b=2, u=1),
                             o[:, :, :, 16:17]).then_inc(d_rs, 1)
                dve.wait_ge(d_rs, n + 1)
                if n >= 2:
                    dve.wait_ge(pe_ot, n - 1)
                for a in range(2):
                    q = slice(a * S, (a + 1) * S)
                    v.tensor_tensor(o_sb[q, i, :, :, a, :], o[q, :, :, a * HD:(a + 1) * HD],
                                    rsum[q, i, :].rearrange("q (b p u) -> q b p u", b=2, u=1)
                                    .to_broadcast([S, 2, NP, HD]), ALU.mult).then_inc(d_o, 1)

            def add_res(n):
                s, t, i = n // NT, n % NT, n % 2
                dve.wait_ge(pe_y, n + 1)
                if s < 2:
                    dve.wait_ge(c_resb, 1 if s == 0 else t + 2)
                    if n >= 2:
                        dve.wait_ge(d_x, n - 1)
                    v.tensor_tensor(res[:, i, :], ps_y[:, P:2 * P], res_b[:, s, t, :], ALU.add).then_inc(d_res, 1)
                    dve.wait_ge(d_res, n + 1)
                    v.bn_stats(stats[:, i, :], res[:, i, :]).then_inc(d_st, 1)
                    dve.wait_ge(d_st, n + 1)
                    if n >= 2:
                        dve.wait_ge(g_rs, cnt_rs(n - 2))
                    v.bn_aggr(mv[:, i, :], stats[:, i, :]).then_inc(d_mv, 1)
                else:
                    dve.wait_ge(d_x, NT + t + 1)
                    v.tensor_tensor(h3[:, t, :], ps_y[:, P:2 * P], x2[:, t, :], ALU.add).then_inc(d_res, 1)

            def finish(n):
                s, t, i = n // NT, n % NT, n % 2
                dve.wait_ge(g_rs, cnt_rs(n))
                if s < 2:
                    v.tensor_scalar((x1, x2)[s][:, t, :], res[:, i, :], mv[:, i, 0:1], rstd[:, i, 1:2],
                                    ALU.subtract, ALU.mult).then_inc(d_x, 1)
                if s == 1:
                    dve.wait_ge(d_x, n + 1)
                    if t == 0:
                        dve.wait_ge(c_rope, 2)
                    if t >= 1:
                        dve.wait_ge(d_xr, 2 * t)
                    for r, w in ((rope_a, rope_c), (rope_b, rope_s)):
                        v.scalar_tensor_tensor(r[:, :], x2[:, t, :], rstd[:, i, 3:4], w[:, :],
                                               ALU.mult, ALU.mult).then_inc(d_ra, 1)
                    dve.wait_ge(d_ra, 2 * (t + 1))
                    ra = rope_a[:, :].rearrange("q (h e) -> q h e", e=2)
                    rbb = rope_b[:, :].rearrange("q (h e) -> q h e", e=2)
                    half = D // 2
                    v.tensor_tensor(xr[:, t, 0:half], ra[:, :, 0], rbb[:, :, 1], ALU.subtract).then_inc(d_xr, 1)
                    v.tensor_tensor(xr[:, t, half:D], rbb[:, :, 0], ra[:, :, 1], ALU.add).then_inc(d_xr, 1)
                if s == 2:
                    v.scalar_tensor_tensor(xm[:, t, :], h3[:, t, :], rstd[:, i, 1:2], w_norm[:, 1, :],
                                           ALU.mult, ALU.mult).then_inc(d_xm, 1)

            v.memset(vbd[:, :, :, :, :, :], 0.0).then_inc(c_zero, 1)
            v.memset(o_sb[:, :, :, :, :, :], 0.0).then_inc(c_zero, 1)
            dve.wait_ge(c_zero, 2)
            v.memset(vbd[0:S, :, :, :, 0, 16:17], 1.0).then_inc(c_zero, 1)
            v.memset(vbd[S:P, :, :, :, 1, 16:17], 1.0).then_inc(c_zero, 1)
            v.memset(ones_bf[:, :], 1.0).then_inc(c_zero, 1)
            v.memset(bias_col[:, 2, :], 0.0).then_inc(c_zero, 1)
            v.memset(eo[:, :, :], 0.0).then_inc(c_zero, 1)
            v.memset(all1_bf[:, :], 1.0).then_inc(c_hot, 1)
            dve.wait_ge(in_cst, 16)
            v.tensor_copy(ident_bf[:, :], ident).then_inc(c_bf, 1)
            v.tensor_copy(mask_bf[:, :], cst[:, C_MASK:C_MASK + 512]).then_inc(c_bf, 1)
            v.tensor_copy(tri_bf[:, :], cst[:, C_TRI:C_TRI + P]).then_inc(c_hot, 1)
            v.tensor_copy(iota_bf[:, :], cst[:, C_IOTA:C_IOTA + P]).then_inc(c_hot, 1)
            dve.wait_ge(in_w, 32)
            wv = w_raw[:, :].rearrange("e (h c d) -> e c h d", c=3, d=HD)
            for c, w in enumerate((w_q, w_k, w_v)):
                v.tensor_copy(w[:, 0, :].rearrange("e (h d) -> e h d", d=HD), wv[:, c]).then_inc(c_wq, 1)
            copy_v(0)
            copy_v(1)
            for it in range(STEPS + 3):
                if 2 <= it < STEPS + 2:
                    norm_o(it - 2)
                if it >= 3:
                    add_res(it - 3)
                if it < STEPS:
                    row_max(it, 0)
                    minus_max(it, 0)
                    row_max(it, 1)
                    minus_max(it, 1)
                if it + 2 < STEPS:
                    copy_v(it + 2)
                if it >= 3:
                    finish(it - 3)

            chain = [0]

            def link(ins):
                chain[0] += 1
                ins.then_inc(d_rt, 1)
                dve.wait_ge(d_rt, chain[0])

            dve.wait_ge(pe_lg, 2)
            full = [P, NT, NE]
            lg = logit[:, :, :]

            def bc(ap):
                return ap.rearrange("q (t u) -> q t u", u=1).to_broadcast(full)

            dve.wait_ge(in_moe, MOE_LOADS)
            v.tensor_tensor(lg, ps_qkv[:, 0:NT * NE].rearrange("q (t e) -> q t e", e=NE),
                            rb[:, :].rearrange("q (u e) -> q u e", u=1).to_broadcast(full),
                            ALU.add).then_inc(d_lg, 1)
            dve.wait_ge(d_lg, 1)
            order = cst[:, C_ORD:C_ORD + NE].rearrange("q (u e) -> q u e", u=1).to_broadcast(full)

            def pick(src, vmax, one_hot):
                link(v.tensor_reduce(vmax, src, AX.X, ALU.max))
                link(v.tensor_tensor(rt[:, 0, :, :], src, bc(vmax), ALU.is_equal))
                link(v.tensor_tensor(rt[:, 1, :, :], rt[:, 0, :, :], order, ALU.mult))
                link(v.tensor_reduce(rv[:, 7, :], rt[:, 1, :, :], AX.X, ALU.max))
                link(v.tensor_tensor(one_hot, rt[:, 1, :, :], bc(rv[:, 7, :]), ALU.is_equal))

            pick(lg, rv[:, 0, :], rt[:, 2, :, :])
            link(v.scalar_tensor_tensor(rt[:, 3, :, :], rt[:, 2, :, :], -3.0e38, lg, ALU.mult, ALU.add))
            pick(rt[:, 3, :, :], rv[:, 1, :], rt[:, 4, :, :])
            link(v.tensor_tensor(rv[:, 2, :], rv[:, 1, :], rv[:, 0, :], ALU.subtract))
            assert chain[0] == RT_EXP, chain
            v.tensor_tensor(sel[:, :, :], rt[:, 2, :, :], rt[:, 4, :, :], ALU.add).then_inc(d_sel, 1)
            dve.wait_ge(pe_rank, 1)
            pairs8 = [P, NE, NE]

            def rows(c, n):
                return cst[:, c:c + n].rearrange("q (u e) -> q u e", u=1)

            link(v.tensor_tensor(over[:, :, :],
                                 bank[6][:, NT * NE:NT * NE + NE].rearrange("q (e u) -> q e u", u=1).to_broadcast(pairs8),
                                 rows(C_K, NE).to_broadcast(pairs8), ALU.is_gt))
            link(v.tensor_reduce(n_tiles[:, :], over[:, :, :], AX.X, ALU.add))
            link(v.tensor_tensor(over[:, :, :], rows(C_LT, NE * NE).rearrange("q u (e f) -> q (u e) f", f=NE),
                                 n_tiles[:, :].rearrange("q (u e) -> q u e", u=1).to_broadcast(pairs8), ALU.mult))
            link(v.tensor_reduce(first[:, :], over[:, :, :], AX.X, ALU.add))
            link(v.scalar_tensor_tensor(dest[:, :, :], first[:, :].rearrange("q (u e) -> q u e", u=1).to_broadcast(full),
                                        float(P), bank[6][:, 0:NT * NE].rearrange("q (t e) -> q t e", e=NE),
                                        ALU.mult, ALU.add))
            both = [P, 2, NT, NE]
            link(v.tensor_tensor(rt[:, 0:2, :, :], rt[:, 2:6:2, :, :],
                                 dest[:, :, :].rearrange("q (u t) e -> q u t e", u=1).to_broadcast(both), ALU.mult))
            link(v.tensor_reduce(slot_f[:, :, :], rt[:, 0:2, :, :], AX.X, ALU.add))
            sf = slot_f[:, :, :].rearrange("q k t -> q (k t)")
            si = slot_i[:, :, :].rearrange("q k t -> q (k t)")
            link(v.tensor_copy(si, sf))
            link(v.tensor_scalar(part_i[:, 0, :], si, P - 1, None, ALU.bitwise_and))
            link(v.tensor_scalar(part_i[:, 1, :], si, 7, None, ALU.logical_shift_right))
            link(v.tensor_copy(part_f[:, :, :], part_i[:, :, :]))
            hot = [P, 2 * NT, NG]
            link(v.tensor_tensor(hi_hot[:, :, :], rows(C_J, NG).to_broadcast(hot),
                                 part_f[:, 1, :].rearrange("q (c u) -> q c u", u=1).to_broadcast(hot), ALU.is_equal))
            v.tensor_scalar(hi_p[:, :, :], hi_hot[:, :, :], cst[:, C_P:C_P + 1], None, ALU.mult).then_inc(d_hot, 1)
            v.tensor_tensor(hi_t[:, :, :], hi_hot[:, :, :],
                            cst[:, C_T:C_T + 2 * NT].rearrange("q (c u) -> q c u", u=1).to_broadcast(hot),
                            ALU.mult).then_inc(d_hot, 1)
            dve.wait_ge(c_hot, 3)
            for c in range(2 * NT):
                v.tensor_scalar(lo_hot[:, c, :], iota_bf[:, :], part_f[:, 0, c:c + 1], None,
                                ALU.is_equal).then_inc(d_hot, 1)
            dve.wait_ge(pe_tok, 1)
            v.tensor_copy(tok_i[:, :], bank[7][:, 0:NG]).then_inc(d_tok, 1)
            ex = [1, NJ, NE]
            link(v.tensor_tensor(ex_f[:, :, :], first[0:1, :].rearrange("q (u e) -> q u e", u=1).to_broadcast(ex),
                                 cst[0:1, C_J:C_J + NJ].rearrange("q (j u) -> q j u", u=1).to_broadcast(ex), ALU.is_le))
            link(v.tensor_reduce(ex_n[:, :], ex_f[:, :, :], AX.X, ALU.add))
            link(v.tensor_scalar(ex_n[:, :], ex_n[:, :], -1.0, None, ALU.add))
            ex_pair = ex_n[:, :].rearrange("o (i u) -> o i u", u=2)
            link(v.scalar_tensor_tensor(quad_f[:, 0, :], ex_pair[:, :, 1], float(NE), ex_pair[:, :, 0],
                                        ALU.mult, ALU.add))
            link(v.scalar_tensor_tensor(quad_f[:, 1, 0:NJ // 2 - 1], quad_f[:, 0, 1:NJ // 2], float(NE * NE),
                                        quad_f[:, 0, 0:NJ // 2 - 1], ALU.mult, ALU.add))
            link(v.tensor_copy(quad_i[:, 0:NJ // 2 - 1], quad_f[:, 1, 0:NJ // 2 - 1]))
            link(v.scalar_tensor_tensor(last_i[:, 1:2], first[0:1, NE - 1:NE], -1.0, n_tiles[0:1, NE - 1:NE],
                                        ALU.add, ALU.add))
            v.tensor_scalar(last_i[:, 0:1], last_i[:, 1:2], 1, None, ALU.logical_shift_right).then_inc(d_ex, 1)
            dve.wait_ge(a_rt, 1)
            link(v.tensor_scalar(rv[:, 4, :], rv[:, 3, :], 1.0, None, ALU.add))
            link(v.reciprocal(rv[:, 5, :], rv[:, 4, :]))
            link(v.tensor_tensor(rv[:, 6, :], rv[:, 3, :], rv[:, 5, :], ALU.mult))

            ps_h2, ps_e = [bank[1], bank[3]], [bank[5], bank[6]]

            def take_slots(j):
                v.tensor_scalar(xs[:, :, :], xg[:, bass.ds(j, 2), :], 0.0, None, ALU.add).then_inc(d_xs, 1)

            def hidden(u):
                v.tensor_tensor(hh[:, u, :], ps_h2[u][:, :], silu[:, u, :], ALU.mult).then_inc(d_hh, 1)

            def keep_out(u, j):
                v.tensor_scalar(eo[:, bass.ds(j, 1), :].rearrange("q a e -> q (a e)"), ps_e[u][:, 0:D],
                                0.0, None, ALU.add).then_inc(d_eo, 1)

            dve.wait_ge(g_gather, 32)
            take_slots(0)
            dve.wait_ge(g_gather, 64)
            dve.wait_ge(pe_xgt, 1)
            take_slots(2)
            for u in range(2):
                dve.wait_ge(a_silu, u + 1)
                dve.wait_ge(pe_h, 2 * u + 2)
                hidden(u)
            dve.wait_ge(y_zero, 16)
            dve.wait_ge(d_ex, 1)
            last = dve.value_load(last_i[0:1, 0:1], min_val=NT - 1, max_val=NJ // 2 - 1)
            with dve.Fori(0, last) as i:
                dve.wait_ge(g_gather, 32 * i + 96)
                dve.wait_ge(pe_xgt, i + 2)
                take_slots(2 * i + 4)
                dve.wait_ge(a_silu, 2 * i + 3)
                dve.wait_ge(pe_h, 4 * i + 6)
                dve.wait_ge(pe_ht, 2 * i + 1)
                hidden(0)
                dve.wait_ge(pe_e, 2 * i + 1)
                keep_out(0, 2 * i)
                dve.wait_ge(pe_e, 2 * i + 2)
                keep_out(1, 2 * i + 1)
                dve.wait_ge(a_silu, 2 * i + 4)
                dve.wait_ge(pe_h, 4 * i + 8)
                dve.wait_ge(pe_ht, 2 * i + 2)
                hidden(1)
            for u in range(2):
                dve.wait_ge(pe_e, 2 * last + 1 + u)
                keep_out(u, 2 * last + u)

            fin = [2 * NT]

            def step(ins):
                fin[0] += 1
                ins.then_inc(d_st, 1)
                dve.wait_ge(d_st, fin[0])

            def normalise(t):
                dve.wait_ge(g_frs, 1 if t < NT - 1 else 2)
                v.tensor_scalar(y_out[:, t, :], acc[:, t, :], fmv[:, t, 0:1], frstd[:, t, 1:2],
                                ALU.subtract, ALU.mult).then_inc(d_fin, 1)

            dve.wait_ge(c_base, NT)
            for t in range(NT):
                if t == NT - 1:
                    for n in range(NT // 2):
                        normalise(n)
                dve.wait_ge(g_yg[t], 32)
                step(v.scalar_tensor_tensor(acc[:, t, :], yg[:, 2 * t, :], rv[:, 5, t:t + 1], base[:, t, :],
                                            ALU.mult, ALU.add))
                step(v.scalar_tensor_tensor(acc[:, t, :], yg[:, 2 * t + 1, :], rv[:, 6, t:t + 1], acc[:, t, :],
                                            ALU.mult, ALU.add))
                step(v.bn_stats(fstats[:, t, :], acc[:, t, :]))
                v.bn_aggr(fmv[:, t, :], fstats[:, t, :]).then_inc(d_fmv, 1)
            for n in range(NT // 2, NT):
                normalise(n)


def _consts():
    c = np.zeros((P, C_END), np.float32)
    r = np.arange(P)
    c[:, C_ID:C_ID + P] = np.eye(P)
    c[r, C_I2 + r % S] = 1
    q, k = r[:, None] % S, np.arange(512)[None, :] % S
    c[:, C_MASK:C_MASK + 512] = np.where(k <= q, 0.0, -1e30)
    half = P // 2
    theta = (np.float32(1.0) / np.float32(10000.0) ** (np.arange(half, dtype=np.float32) / np.float32(half)))
    ang = (r % S).astype(np.float32)[:, None] * theta[None, :].astype(np.float32)
    c[:, C_COS:C_COS + P] = np.repeat(np.cos(ang), 2, axis=1)
    c[:, C_SIN:C_SIN + P] = np.repeat(np.sin(ang), 2, axis=1)
    c[r, C_MA + (r // HD) % 2] = 1
    c[r, C_M8 + r // (2 * HD)] = 1
    c[:, C_IOTA:C_IOTA + P] = r
    c[:, C_TRI:C_TRI + P] = r[:, None] < r[None, :]
    c[:, C_J:C_J + NG] = np.arange(NG)
    c[:, C_K:C_K + NE] = P * np.arange(NE)
    e = np.arange(NE)
    c[:, C_LT:C_LT + NE * NE] = (e[None, :] < e[:, None]).ravel()
    c[:, C_P] = r
    c[:, C_T:C_T + 2 * NT] = P * (np.arange(2 * NT) % NT)
    c[:, C_ORD:C_ORD + NE] = NE - e
    return c


def kernel(**inputs):
    import concourse.bacc as bacc
    from concourse.bass_utils import run_bass_kernel_spmd

    nc = bacc.Bacc("TRN2", target_bir_lowering=False, num_devices=1)
    arrays, t_in = {}, {}
    for name, a in inputs.items():
        a = np.ascontiguousarray(a)
        arrays["in_" + name] = a
        t_in[name] = nc.dram_tensor("in_" + name, a.shape, mybir.dt.from_np(a.dtype), kind="ExternalInput").ap()
    arrays["in_consts"] = _consts()
    consts = nc.dram_tensor("in_consts", (P, C_END), F32, kind="ExternalInput").ap()
    out = nc.dram_tensor("out", (B, S, D), F32, kind="ExternalOutput").ap()
    decoder_kernel(nc, t_in, consts, out)
    r = run_bass_kernel_spmd(nc, [arrays], core_ids=[0])
    return r.results[0]["out"]
```
